# Optimizing a Trainium2 kernel written in Bass

```python
import numpy as np
import jax
import jax.numpy as jnp

def _softmax(x, axis=-1):
    return jax.nn.softmax(x, axis=axis)

def _gelu(x):
    return jax.nn.gelu(x, approximate=True)

def _silu(x):
    return jax.nn.silu(x)

def _sigmoid(x):
    return jax.nn.sigmoid(x)

def _layernorm(x, axis=-1, eps=1e-05):
    m = jnp.mean(x, axis=axis, keepdims=True)
    v = jnp.var(x, axis=axis, keepdims=True)
    return (x - m) / jnp.sqrt(v + eps)

def _scatter_add(tgt, idx, src, axis=0):
    return tgt.at[idx].add(src)

def _segment_sum(src, seg, n):
    return jax.ops.segment_sum(src, seg, n)
kernel_name = 'mk_adaln_ffn_d1_seqx_r2_bef02c'

def setup_inputs(seed: int=0):
    np.random.seed(seed)
    _w = jnp.asarray

    def _rec_inputs():
        import jax
        import jax.numpy as jnp
        _rk = jax.random.key(seed)
        x = -0.000125 + 0.9999 * jax.random.normal(jax.random.fold_in(_rk, 1), (8, 512, 2048), jnp.float32)
        _lenS = 512 - jax.random.randint(jax.random.fold_in(_rk, 7), (8,), 0, max(1, 512 // 4) + 1, jnp.int32)
        _lenS2 = 512 - jax.random.randint(jax.random.fold_in(_rk, 8), (8,), 0, max(1, 512 // 4) + 1, jnp.int32)
        itok_B_3_7 = jax.random.randint(jax.random.fold_in(_rk, 11), (8,), 3, 8, jnp.int32)
        return (x, itok_B_3_7)
    x, itok_B_3_7 = _rec_inputs()

    def _L0_cond_setup():
        import jax, jax.numpy as jnp
        import numpy as np
        RANK = 16
        ALPHA = 16.0
        SCALING = ALPHA / RANK
        N_ADAPTERS = 8
        IN_F = 2048
        OUT_F = 2048
        BATCH = 4
        SEQ = 1024
        key = jax.random.key(seed)
        kx, ka, kb, ki = jax.random.split(key, 4)
        x = jax.random.normal(kx, (BATCH, SEQ, IN_F), dtype=jnp.float32)
        A = jax.random.normal(ka, (N_ADAPTERS, OUT_F, RANK), dtype=jnp.float32) * 0.02
        B = jax.random.normal(kb, (N_ADAPTERS, RANK, IN_F), dtype=jnp.float32) * 0.02
        adapter_ids = jax.random.randint(ki, (BATCH,), 0, N_ADAPTERS, dtype=jnp.int32)
        return {'x': x, 'A': A, 'B': B, 'adapter_ids': adapter_ids}
    _L0_cond_all = _L0_cond_setup()
    _L0_cond_in = {k: v for k, v in _L0_cond_all.items() if k in ('A', 'B')}
    del _L0_cond_all

    def _L0_ffn_setup():
        import jax, jax.numpy as jnp
        import numpy as np
        TOP_K = 2
        SCALING = 32.0 / 64.0
        key = jax.random.key(seed)
        ks = jax.random.split(key, 6)
        Bsz, S, Din, Dout, R, E = (4, 1024, 2048, 2048, 64, 16)
        x = jax.random.normal(ks[0], (Bsz, S, Din), dtype=jnp.float32)
        base_w = jax.random.normal(ks[1], (Dout, Din), dtype=jnp.float32) * 0.02
        base_b = jax.random.normal(ks[2], (Dout,), dtype=jnp.float32) * 0.02
        A = jax.random.normal(ks[3], (R, Din), dtype=jnp.float32) * (1.0 / np.sqrt(Din))
        B = jax.random.normal(ks[4], (E, Dout, R), dtype=jnp.float32) * 0.02
        router_w = jax.random.normal(ks[5], (E, Din), dtype=jnp.float32) * 0.02
        return {'x': x, 'base_w': base_w, 'base_b': base_b, 'A': A, 'B': B, 'router_w': router_w}
    _L0_ffn_all = _L0_ffn_setup()
    _L0_ffn_in = {k: v for k, v in _L0_ffn_all.items() if k in ('base_w', 'base_b', 'A', 'B', 'router_w')}
    del _L0_ffn_all
    return {'x': x, 'itok_B_3_7': itok_B_3_7, 'L0_cond_A': _L0_cond_in['A'], 'L0_cond_B': _L0_cond_in['B'], 'L0_ffn_base_w': _L0_ffn_in['base_w'], 'L0_ffn_base_b': _L0_ffn_in['base_b'], 'L0_ffn_A': _L0_ffn_in['A'], 'L0_ffn_B': _L0_ffn_in['B'], 'L0_ffn_router_w': _L0_ffn_in['router_w']}

def reference(x, itok_B_3_7, L0_cond_A, L0_cond_B, L0_ffn_base_w, L0_ffn_base_b, L0_ffn_A, L0_ffn_B, L0_ffn_router_w):
    import jax
    import jax.numpy as jnp

    def _L0_cond_ref(x, A, B, adapter_ids):
        import jax, jax.numpy as jnp
        import numpy as np
        RANK = 16
        ALPHA = 16.0
        SCALING = ALPHA / RANK
        N_ADAPTERS = 8
        IN_F = 2048
        OUT_F = 2048
        BATCH = 4
        SEQ = 1024
        B_sel = B[adapter_ids]
        A_sel = A[adapter_ids]
        Bx = jnp.einsum('bni,bri->bnr', x, B_sel)
        out = jnp.einsum('bnr,bor->bno', Bx, A_sel)
        return out * SCALING

    def _L0_ffn_ref(x, base_w, base_b, A, B, router_w):
        import jax, jax.numpy as jnp
        import numpy as np
        TOP_K = 2
        SCALING = 32.0 / 64.0
        base_out = jnp.einsum('bsi,oi->bso', x, base_w) + base_b
        res_hidden = jnp.einsum('bsi,ri->bsr', x, A)
        logits = jnp.einsum('bsi,ei->bse', x, router_w)
        probs = jax.nn.softmax(logits, axis=-1)
        topw, topi = jax.lax.top_k(probs, TOP_K)
        topw = topw / (jnp.sum(topw, axis=-1, keepdims=True) + 1e-06)
        num_experts = B.shape[0]
        combine = jnp.sum(jax.nn.one_hot(topi, num_experts, dtype=x.dtype) * topw[..., None], axis=-2)
        delta = jnp.einsum('bse,bsr,eor->bso', combine, res_hidden, B)
        return base_out + delta * SCALING
    x = x + _L0_ffn_ref(_L0_cond_ref(x, L0_cond_A, L0_cond_B, itok_B_3_7), L0_ffn_base_w, L0_ffn_base_b, L0_ffn_A, L0_ffn_B, L0_ffn_router_w)
    return x

_drawn_inputs = setup_inputs


def setup_inputs(seed=0):
    import zlib

    import numpy as np

    out = dict(_drawn_inputs(seed))
    spreads = {}
    factors = {'L0_ffn_base_b': 2.768, 'L0_ffn_A': 8.0, 'L0_ffn_B': 8.0, 'L0_ffn_router_w': 8.0}
    for name, (base, spread) in spreads.items():
        noise = np.random.default_rng([zlib.crc32(name.encode()), seed]).standard_normal(out[name].shape)
        drawn = base * np.exp(spread * noise) if base else spread * noise
        out[name] = jnp.asarray(drawn.astype(out[name].dtype))
    for name, factor in factors.items():
        out[name] = (out[name] * factor).astype(out[name].dtype)
    return out
```

```python
from contextlib import ExitStack

import concourse.bass as bass
from concourse import mybir

F32 = mybir.dt.float32
F32R = mybir.dt.float32r
I32 = mybir.dt.int32
U32 = mybir.dt.uint32
ALU = mybir.AluOpType
ACT = mybir.ActivationFunctionType
AX = mybir.AxisListType

P = 128
BANK = 512
RING = 4


def adaln_ffn(nc, x, itok, cond_A, cond_B, base_w, base_b, ffn_A, ffn_B, router_w, out):
    NB, T, D = x.shape
    NAD, _, RK = cond_A.shape
    E, O, R = ffn_B.shape
    NT = T // P
    NC = D // BANK
    KD = D // P
    KC = KD // NC
    OC = O // BANK
    EH = E // 2
    NP = E // 2
    MT = OC * NT
    assert T == BANK and NB * RK == P and 2 * R == P and EH * RK == P and D == O
    W_GROUPS = O // (NT * P)
    B_GROUPS = 2
    X_GROUP0 = W_GROUPS + B_GROUPS
    TB_S, TB_R, TB = D // P * RK, D // P * RK + 2 * RK, D // P * RK + 3 * RK

    x_v = x.rearrange("b (t p) d -> b p t d", p=P)
    out_v = out.rearrange("b (t p) d -> b p t d", p=P)
    w_v = base_w.rearrange("(g t p) d -> g p t d", t=NT, p=P)
    bexp_v = ffn_B.rearrange("e (c t p) r -> c t p e r", t=NT, p=P)
    condA_v = cond_A.rearrange("n (c p s) k -> n p c (s k)", p=P, s=KC)

    with ExitStack() as ctx:
        def sb(name, shape, dt=F32):
            return ctx.enter_context(nc.sbuf_tensor(name, shape, dt))

        def sem(name):
            return ctx.enter_context(nc.semaphore(name))

        g_dram = nc.dram_tensor("g_hilo", (2, P, O), F32, kind="Internal").ap()

        xbuf = [sb(f"xbuf{q}", [P, NT, D]) for q in range(2)]
        bexpT = sb("bexpT", [P, NP, O])
        h_r = sb("h_r", [P, 2, 2, 2, BANK], F32R)
        u_r = sb("u_r", [P, 2, 2, 2, T], F32R)
        sbx_r = sb("sbx_r", [P, 2, T], F32R)
        gm_r = sb("gm_r", [P, 2, O], F32R)
        xT = sb("xT", [P, RING, T])
        table = sb("table", [P, NB, TB])
        cur = sb("cur", [P, 2, TB])
        tmp = sb("tmp", [P, 2, T])
        bxp = tmp[:, 0, :]
        bx = sb("bx", [P, T])
        ident = sb("ident", [P, P])
        spread = sb("spread", [P, P])
        iota_e = sb("iota_e", [P, E])
        tok = sb("tok", [1, NB], I32)
        mx = sb("mx", [P, NT])
        ex = sb("ex", [P, NT, E])
        ssum = sb("ssum", [P, NT])
        rs = sb("rs", [P, NT])
        top = sb("top", [P, NT, 8])
        sel = xT[:, 0, 0:NT * 2 * E].rearrange("p (t k e) -> p t k e", t=NT, k=2)
        comb = xT[:, 1, 0:NT * E].rearrange("p (t e) -> p t e", t=NT)
        wt2 = xT[:, 1, 128:128 + 2 * NT].rearrange("p (t k) -> p t k", t=NT)
        topf = xT[:, 1, 256:256 + 2 * NT].rearrange("p (t k) -> p t k", t=NT)
        topi = xT[:, 1, 384:384 + 8 * NT].bitcast(U32).rearrange("p (t k) -> p t k", t=NT)
        combk = xT[:, 2:4, :].rearrange("p a (t e k) -> p (a t) e k", e=E, k=RK)

        flat = bexpT[:, :, :].rearrange("p a o -> p (a o)")
        def carve(at, n):
            return flat[:, at:at + n]
        condb_n = carve(0, D)
        ffna_n = carve(D, D)
        router_n = carve(2 * D, D)
        conda_n = carve(3 * D, D).rearrange("p (b c s k) -> p b c s k", b=NB, c=NC, s=KC)
        ffnaT = carve(4 * D, KD * P).rearrange("p (j m) -> p j m", j=KD)
        routerT = carve(5 * D, KD * E).rearrange("p (j e) -> p j e", j=KD)
        sum16 = carve(5 * D + KD * E, RK)
        grT = carve(7 * D, NB * P)[0:E, :].rearrange("e (b g u k) -> e b g u k", b=NB, u=2, k=RK)
        bias_n = carve(6 * D, O)
        a_r = u_r[:, :, :, :, :].rearrange("p q l h t -> p (q l h t)").rearrange("p (l j m) -> p l j m", l=2, j=KD)
        wT_r = h_r[:, :, :, :, :].rearrange("p s l h o -> p (s l h) o").rearrange("p (n l) o -> p n l o", n=RING)

        ps = ctx.enter_context(nc.psum_tensor("ps", [P, 8, BANK], F32))
        XP, HB, ACC, MISC, BXB = 0, 2, 4, 6, 7

        s_const, s_idn, s_sum, s_iota = sem("const"), sem("idn"), sem("sum16"), sem("iota")
        s_tok, s_conda, s_condb, s_small, s_bias = sem("tok"), sem("conda"), sem("condb"), sem("small"), sem("bias")
        s_load = [[sem(f"load{q}{c}") for c in range(NC)] for q in range(2)]
        s_store = [sem(f"store{c}") for c in range(OC)]
        s_gst, s_gm = sem("g_stored"), [sem("gm0"), sem("gm1")]
        s_biashi, s_biaslo = sem("bias_hi"), sem("bias_lo")
        s_ahi, s_alo = sem("a_hi"), sem("a_lo")
        s_wt, s_whi, s_wlo, s_wmm = sem("w_transposed"), sem("w_hi"), sem("w_lo"), sem("w_used")
        s_ghi, s_glo = sem("g_hi"), sem("g_lo")
        s_st, s_se = sem("small_transposed"), sem("small_copied")
        s_sm, s_grs, s_sel, s_table = sem("ga_gr"), sem("gr_copied"), sem("gr_spread"), sem("table_done")
        s_bt, s_be = sem("b_transposed"), [sem("b_even"), sem("b_odd")]
        s_cur = sem("cur")
        s_xt, s_xe, s_bxq = sem("x_transposed"), sem("xT_copied"), sem("bx_quad")
        s_bxp, s_lg, s_rep, s_bx = sem("bx_partial"), sem("logits"), sem("bx_spread"), sem("bx_copied")
        s_lm, s_exp, s_comb, s_ct = sem("logits_minus_max"), sem("exp"), sem("comb"), sem("comb_transposed")
        s_combk = sem("comb_by_k")
        s_up, s_uhi, s_ulo = sem("u_product"), sem("u_hi"), sem("u_lo")
        s_sbhi, s_sblo = sem("sb_hi"), sem("sb_lo")
        s_h, s_hhi, s_hlo = sem("h_done"), sem("h_hi"), sem("h_lo")
        s_acc, s_out = sem("tile_done"), sem("tile_added")
        s_dve, s_gate = sem("dve_chain"), sem("dve_gate")
        CREDIT = RING
        DVE_PER_FRONT = 17

        def need(eng, s, v):
            if not isinstance(v, int) or v > 0:
                eng.wait_ge(s, v)

        def f32(ap):
            return ap.bitcast(F32)

        class Batch:
            def __init__(self, half, q):
                self.half, self.q, self.n = half, q, half * 2 + q

        def batches(eng, step):
            step(Batch(0, 0), Batch(0, 1))
            with eng.Fori(0, NB // 2 - 1) as i:
                step(Batch(i, 1), Batch(i + 1, 0))
                step(Batch(i + 1, 0), Batch(i + 1, 1))
            step(Batch(NB // 2 - 1, 1), None)

        def copy_b(eng, copy, n):
            g, c, s = n // (4 * NC), n // 4 % NC, n % 4
            oc, pair = 2 * g + c // 2, 4 * (c % 2) + s
            eng.wait_ge(s_bt, n + 1)
            copy(bexpT[:, pair, oc * BANK:(oc + 1) * BANK], ps[:, n % RING, :]).then_inc(s_be[n % 2], 1)

        T_AT = {m: (2 * m, 2 * m + 1) for m in range(8)}
        Q_AT = {2: 0, 4: 1, 6: 2, 8: 3}
        SPREAD_AT, MAX_AT, EXP_AT, TOP_AT, COMB_AT = 9, 9, 10, 11, 12
        CT_AT = {13: 0, 14: 1}
        UP_AT = {14: 0, 15: 1}

        block = ctx.enter_context(nc.Block())

        @block.sync
        def _(sp):
            sp.dma_start(tok[:, :], itok.rearrange("(a b) -> a b", a=1)).then_inc(s_tok, 16)
            sp.wait_ge(s_tok, 16)
            ids = [sp.value_load(tok[0:1, b:b + 1], min_val=0, max_val=NAD - 1) for b in range(NB)]
            for b in range(NB):
                sp.dma_start(conda_n[:, b, :, :, :].rearrange("p c s k -> p c (s k)"),
                             condA_v[ids[b], :, :, :]).then_inc(s_conda, 16)

            def load_w(g, c):
                sp.dma_start(xbuf[g % 2][:, :, c * BANK:(c + 1) * BANK],
                             w_v[g, :, :, c * BANK:(c + 1) * BANK]).then_inc(s_load[g % 2][c], 16)

            def load_b(g, c):
                q, oh, eh = g % 2, c // 2, c % 2
                for t in range(NT):
                    dst = xbuf[q][:, t, c * BANK:(c + 1) * BANK].rearrange("p (e r) -> p e r", r=R)
                    sp.dma_start(dst, bexp_v[2 * (g - W_GROUPS) + oh, t, :, eh * EH:(eh + 1) * EH, :])\
                      .then_inc(s_load[q][c], 16)

            def load_x(b, q, c):
                sp.dma_start(xbuf[q][:, :, c * BANK:(c + 1) * BANK],
                             x_v[b, :, :, c * BANK:(c + 1) * BANK]).then_inc(s_load[q][c], 16)

            for g in range(2):
                for c in range(NC):
                    load_w(g, c)
            for b in range(NB):
                sp.dma_start(condb_n[b * RK:(b + 1) * RK, :], cond_B[ids[b], :, :]).then_inc(s_condb, 16)
            for n in range(2):
                sp.dma_start(ffna_n[n * R:(n + 1) * R, :], ffn_A).then_inc(s_small, 16)
            sp.dma_start(router_n[0:E, :], router_w).then_inc(s_small, 16)
            for row in (64, 96):
                sp.dma_start(bias_n[row:row + 1, :], base_b.rearrange("(a o) -> a o", a=1)).then_inc(s_bias, 16)
            for g in range(2, X_GROUP0 + 2):
                for c in range(NC):
                    if g - 2 < W_GROUPS:
                        sp.wait_ge(s_wt, KD * (g - 2) + KC * (c + 1))
                    else:
                        sp.wait_ge(s_bt, 4 * NC * (g - 2 - W_GROUPS) + 4 * (c + 1))
                    if g < W_GROUPS:
                        load_w(g, c)
                    elif g < X_GROUP0:
                        load_b(g, c)
                    else:
                        load_x(g - X_GROUP0, g % 2, c)
                if g - 2 < W_GROUPS:
                    sp.wait_ge(s_glo, g - 2 + 1 + 2)
                    sp.dma_start(g_dram[:, :, (g - 2) * BANK:(g - 1) * BANK].rearrange("l p o -> p l o"),
                                 tmp[:, :, :]).then_inc(s_gst, 16)

            def load_gm(b, q):
                for rep in range(2):
                    for l in range(2):
                        row = (2 * rep + l) * RK
                        sp.dma_start(f32(gm_r[row:row + RK, q, :]),
                                     g_dram[l, bass.ds(b * RK, RK), :]).then_inc(s_gm[q], 16)

            sp.wait_ge(s_gst, 16 * (W_GROUPS + 1))
            load_gm(0, 0)

            def step(b, f):
                if f is not None:
                    need(sp, s_acc, b.n * MT)
                    load_gm(f.n, f.q)
                for c in range(OC):
                    sp.wait_ge(s_out, b.n * MT + NT * (c + 1))
                    sp.dma_start(out_v[b.n, :, :, c * BANK:(c + 1) * BANK],
                                 xbuf[b.q][:, :, c * BANK:(c + 1) * BANK]).then_inc(s_store[c], 16)
                    if c > 0:
                        reload(b, c - 1)
                reload(b, OC - 1)

            def reload(b, c):
                if isinstance(b.n, int) and b.n + 2 >= NB:
                    return
                sp.wait_ge(s_store[c], b.n * 16 + 16)
                load_x(b.n + 2, b.q, c)

            step(Batch(0, 0), Batch(0, 1))
            with sp.Fori(0, NB // 2 - 2) as i:
                step(Batch(i, 1), Batch(i + 1, 0))
                step(Batch(i + 1, 0), Batch(i + 1, 1))
            h = NB // 2 - 2
            step(Batch(h, 1), Batch(h + 1, 0))
            step(Batch(h + 1, 0), Batch(h + 1, 1))
            step(Batch(h + 1, 1), None)
            for c in range(OC):
                sp.wait_ge(s_store[c], 16 * NB)

        @block.gpsimd
        def _(pool):
            pool.memset(ident[:, :], 0.0).then_inc(s_idn, 1)
            pool.wait_ge(s_idn, 1)
            pool.affine_select(out=ident[:, :], in_=ident[:, :], compare_op=ALU.not_equal, fill=1.0, base=0,
                               pattern=[[-1, P]], channel_multiplier=1).then_inc(s_idn, 1)
            pool.sem_inc(s_wlo, CREDIT)
            pool.sem_inc(s_wmm, CREDIT)
            pool.sem_inc(s_glo, 2)
            pool.sem_inc(s_gst, 16)
            fills = [(grT, 0.0), (table[:, :, :], 0.0), (f32(sbx_r[64:P, :, :]), 1.0), (f32(gm_r[64:P, :, :]), 0.0)]
            pool.wait_ge(s_idn, 2)
            for n, (where, value) in enumerate(fills):
                pool.memset(where, value).then_inc(s_const, 1)
                pool.wait_ge(s_const, n + 1)
            pool.iota(iota_e[:, :], [[1, E]], base=0, channel_multiplier=0,
                      allow_small_or_imprecise_dtypes=True).then_inc(s_iota, 1)
            pool.wait_ge(s_iota, 1)

            def take(f):
                pool.wait_ge(s_se, 9)
                pool.wait_ge(s_table, 3)
                need(pool, s_h, (f.n - 1) * 2 * OC)
                need(pool, s_lg, f.n - 1)
                pool.tensor_copy(cur[:, f.q, :], table[:, f.n, :]).then_inc(s_cur, 1)

            take(Batch(0, 0))

            def step(b, f):
                if f is not None:
                    take(f)
            batches(pool, step)

        @block.scalar
        def _(act):
            def copy(dst, src):
                return act.activation(dst, src, ACT.Copy)

            def by_chunk(ap):
                return ap.rearrange("p b c s k -> p (c s) b k")

            act.wait_ge(s_conda, 16 * NB)
            copy(a_r[:, 0, :, :].rearrange("p j (b k) -> p j b k", b=NB), by_chunk(conda_n)).then_inc(s_ahi, 1)
            act.wait_ge(s_bias, 32)
            act.wait_ge(s_const, 4)
            for q in range(2):
                for row in (64, 96):
                    copy(gm_r[row:row + 1, q, :], bias_n[row:row + 1, :]).then_inc(s_biashi, 1)

            with act.Fori(0, W_GROUPS // 2) as i:
                for q in range(2):
                    g = i * 2 + q
                    for j in range(KD):
                        n = g * KD + j
                        act.wait_ge(s_wt, n + 1)
                        act.wait_ge(s_wmm, n - RING + 1 + CREDIT)
                        copy(wT_r[:, j % RING, 0, :], ps[:, j % RING, :]).then_inc(s_whi, 1)
                    act.wait_ge(s_wmm, (g + 1) * KD + CREDIT)
                    act.wait_ge(s_gst, g * 16 + 16)
                    copy(tmp[:, 0, :].bitcast(F32R), ps[:, ACC + q, :]).then_inc(s_ghi, 1)

            for n in range(0, 4 * NC * B_GROUPS, 2):
                copy_b(act, copy, n)

            def h_hi(b, c):
                for h in range(2):
                    act.wait_ge(s_h, (b.n * OC + c) * 2 + h + 1)
                    if h == 0:
                        need(act, s_acc, (b.n * OC + c - 1) * NT)
                    copy(h_r[:, c % 2, 0, h, :], ps[:, HB + h, :]).then_inc(s_hhi, 1)

            def slot(f, m):
                for j in T_AT.get(m, ()):
                    n = f.n * KD + j
                    act.wait_ge(s_xt, n + 1)
                    if j % 4 == 0:
                        need(act, s_bxq, f.n * NC + j // 4)
                    if j == 0:
                        need(act, s_ct, f.n * 2)
                    copy(xT[:, j % RING, :], ps[:, XP + j % 2, :]).then_inc(s_xe, 1)
                if m == 8:
                    act.wait_ge(s_bxq, f.n * NC + NC)
                    need(act, s_ulo, f.n * 2)
                    copy(bxp, ps[:, BXB, :]).then_inc(s_bxp, 1)
                if m == SPREAD_AT:
                    act.wait_ge(s_rep, f.n + 1)
                    need(act, s_up, f.n * 2)
                    copy(bx[:, :], ps[:, BXB, :]).then_inc(s_bx, 1)
                    act.wait_ge(s_bx, f.n + 1)
                    need(act, s_acc, (f.n - 1) * MT)
                    copy(sbx_r[0:64, f.q, :], bx[0:64, :]).then_inc(s_sbhi, 1)
                if m == EXP_AT:
                    act.wait_ge(s_lm, f.n + 1)
                    act.activation(ex[:, :, :], ex[:, :, :], ACT.Exp).then_inc(s_exp, 1)
                if m == COMB_AT:
                    act.wait_ge(s_comb, f.n + 1)
                    for a in range(2):
                        copy(combk[:, 2 * a:2 * a + 2].rearrange("p t e k -> p (t e) k"),
                             comb[:, 2 * a:2 * a + 2].rearrange("p t e -> p (t e)").unsqueeze(2)
                             .to_broadcast([P, 2 * E, RK])).then_inc(s_combk, 1)
                if m in UP_AT:
                    h = UP_AT[m]
                    act.wait_ge(s_up, f.n * 2 + h + 1)
                    copy(u_r[:, f.q, 0, h, :], tmp[:, h, :]).then_inc(s_uhi, 1)

            act.wait_ge(s_gst, 16 * (W_GROUPS + 1))
            first = Batch(0, 0)
            for m in range(MT):
                slot(first, m)
            h_hi(first, 0)

            def step(b, f):
                for c in range(OC):
                    if c < OC - 1:
                        h_hi(b, c + 1)
                    elif f is not None:
                        h_hi(f, 0)
                    for t in range(NT):
                        if f is not None:
                            slot(f, c * NT + t)
            batches(act, step)

        @block.vector
        def _(dve):
            dve.wait_ge(s_idn, 2)
            dve.tensor_reduce(sum16, ident[:, :].rearrange("p (g u k) -> p u k g", u=2, k=RK)[:, 0], AX.X, ALU.add)\
               .then_inc(s_sum, 1)
            dve.wait_ge(s_sum, 1)
            dve.tensor_copy(spread[:, :].rearrange("p (g k) -> p g k", k=RK),
                            sum16.unsqueeze(1).to_broadcast([P, P // RK, RK])).then_inc(s_sum, 1)
            dve.wait_ge(s_ahi, 1)
            by_b = a_r[:, :, :, :].rearrange("p l j (b k) -> p l j b k", b=NB)
            dve.tensor_tensor(by_b[:, 1], conda_n.rearrange("p b c s k -> p (c s) b k"), f32(by_b[:, 0]),
                              ALU.subtract).then_inc(s_alo, 1)
            dve.wait_ge(s_biashi, 4)
            for q in range(2):
                dve.tensor_tensor(gm_r[96:97, q, :], bias_n[96:97, :], f32(gm_r[96:97, q, :]), ALU.subtract)\
                   .then_inc(s_biaslo, 1)

            with dve.Fori(0, W_GROUPS // 2) as i:
                for q in range(2):
                    g = i * 2 + q
                    for j in range(KD):
                        n = g * KD + j
                        dve.wait_ge(s_whi, n + 1)
                        dve.tensor_tensor(wT_r[:, j % RING, 1, :], ps[:, j % RING, :],
                                          f32(wT_r[:, j % RING, 0, :]), ALU.subtract).then_inc(s_wlo, 1)
                    dve.wait_ge(s_ghi, g + 1)
                    dve.tensor_tensor(tmp[:, 1, :].bitcast(F32R), ps[:, ACC + q, :], tmp[:, 0, :], ALU.subtract)\
                       .then_inc(s_glo, 1)

            tb = table[:, :, 0:KD * RK].rearrange("p b (j k) -> p j b k", k=RK)
            dve.wait_ge(s_const, 4)
            for n in range(9):
                dve.wait_ge(s_st, n + 1)
                bank = ps[:, n % RING, :]
                if n < 4:
                    dst, src = tb[:, 4 * n:4 * n + 4], bank.rearrange("p (j b k) -> p j b k", j=4, b=NB)
                elif n < 8:
                    dst, src = ffnaT[:, 4 * (n - 4):4 * (n - 3), :], bank.rearrange("p (j m) -> p j m", j=4)
                else:
                    dst, src = routerT, bank[:, 0:KD * E].rearrange("p (j e) -> p j e", e=E)
                dve.tensor_copy(dst, src).then_inc(s_se, 1)
            dve.wait_ge(s_sm, 1)
            ga = ps[:, MISC, 0:P].rearrange("p (b k) -> p b k", b=NB)
            for n in range(2):
                dve.tensor_scalar(table[n * R:(n + 1) * R, :, TB_S + n * RK:TB_S + (n + 1) * RK],
                                  ga[n * R:(n + 1) * R], 0.5, None, ALU.mult).then_inc(s_table, 1)
            dve.wait_ge(s_sm, 2)
            for g in range(P // (2 * RK)):
                dve.tensor_copy(grT[:, :, g, 0, :], ps[0:E, BXB, 0:P].rearrange("p (b k) -> p b k", b=NB))\
                   .then_inc(s_grs, 1)
            dve.wait_ge(s_sel, 1)
            dve.tensor_copy(table[:, :, TB_R:TB_R + E], ps[:, MISC, 0:NB * E].rearrange("p (b e) -> p b e", b=NB))\
               .then_inc(s_table, 1)

            for n in range(1, 4 * NC * B_GROUPS, 2):
                copy_b(dve, dve.tensor_copy, n)

            def h_lo(b, c):
                for h in range(2):
                    dve.wait_ge(s_hhi, (b.n * OC + c) * 2 + h + 1)
                    dve.tensor_tensor(h_r[:, c % 2, 1, h, :], ps[:, HB + h, :], f32(h_r[:, c % 2, 0, h, :]),
                                      ALU.subtract).then_inc(s_hlo, 1)

            def slot(f, m):
                base = f.n * DVE_PER_FRONT
                at = {MAX_AT: 0, TOP_AT: 1, COMB_AT: 10}.get(m, 0)
                count = [at]

                def link(ins):
                    count[0] += 1
                    return ins.then_inc(s_dve, 1)

                def after(n=None):
                    dve.wait_ge(s_dve, base + (count[0] if n is None else n))

                def wide(ap):
                    return ap.unsqueeze(2).to_broadcast([P, NT, E])

                if m == MAX_AT:
                    dve.wait_ge(s_lg, f.n + 1)
                    lg = ps[:, MISC, 0:NT * E].rearrange("p (t e) -> p t e", t=NT)
                    link(dve.tensor_reduce(mx[:, :], lg, AX.X, ALU.max))
                    after()
                    dve.tensor_tensor(ex[:, :, :], lg, wide(mx[:, :]), ALU.subtract).then_inc(s_lm, 1)
                if m == TOP_AT:
                    dve.wait_ge(s_exp, f.n + 1)
                    link(dve.tensor_reduce(ssum[:, :], ex[:, :, :], AX.X, ALU.add))
                    after()
                    link(dve.reciprocal(rs[:, :], ssum[:, :]))
                    after()
                    link(dve.tensor_tensor(ex[:, :, :], ex[:, :, :], wide(rs[:, :]), ALU.mult))
                    after()
                    dve.sem_inc(s_gate, 1)
                    for t in range(NT):
                        link(dve.max(top[:, t, :], ex[:, t, :]))
                    after()
                    dve.sem_inc(s_gate, 1)
                    for t in range(NT):
                        ins = dve.max_index(topi[:, t, :], top[:, t, :], ex[:, t, :])
                        if t == NT - 1:
                            link(ins)
                    link(dve.scalar_tensor_tensor(out=rs[:, :], in0=top[:, :, 0], scalar=1e-6, in1=top[:, :, 1],
                                                  op0=ALU.add, op1=ALU.add))
                if m == COMB_AT:
                    after()
                    link(dve.reciprocal(ssum[:, :], rs[:, :]))
                    link(dve.tensor_copy(topf[:, :, :], topi[:, :, 0:2]))
                    after()
                    link(dve.tensor_tensor(wt2[:, :, :], top[:, :, 0:2],
                                           ssum[:, :].unsqueeze(2).to_broadcast([P, NT, 2]), ALU.mult))
                    iota_w = iota_e[:, :].unsqueeze(1).to_broadcast([P, NT, E])
                    for k in range(2):
                        link(dve.tensor_tensor(sel[:, :, k, :], iota_w, wide(topf[:, :, k]), ALU.is_equal))
                    after()
                    for k in range(2):
                        link(dve.tensor_tensor(sel[:, :, k, :], sel[:, :, k, :], wide(wt2[:, :, k]), ALU.mult))
                    after()
                    dve.tensor_tensor(comb[:, :, :], sel[:, :, 0, :], sel[:, :, 1, :], ALU.add).then_inc(s_comb, 1)
                    dve.wait_ge(s_sbhi, f.n + 1)
                    dve.tensor_tensor(sbx_r[32:64, f.q, :], bx[32:64, :], f32(sbx_r[32:64, f.q, :]), ALU.subtract)\
                       .then_inc(s_sblo, 1)
                if m in UP_AT:
                    h = UP_AT[m]
                    dve.wait_ge(s_ct, f.n * 2 + h + 1)
                    need(dve, s_uhi, f.n * 2 - 2 + h + 1)
                    dve.tensor_tensor(tmp[:, h, :], ps[:, (MISC, BXB)[h], :], bx[:, :], ALU.mult).then_inc(s_up, 1)
                if m == MT - 1:
                    for h in range(2):
                        dve.wait_ge(s_uhi, f.n * 2 + h + 1)
                        dve.tensor_tensor(u_r[:, f.q, 1, h, :], tmp[:, h, :], f32(u_r[:, f.q, 0, h, :]),
                                          ALU.subtract).then_inc(s_ulo, 1)

            first = Batch(0, 0)
            for m in range(MT):
                slot(first, m)
            h_lo(first, 0)

            def step(b, f):
                for c in range(OC):
                    if c < OC - 1:
                        h_lo(b, c + 1)
                    elif f is not None:
                        h_lo(f, 0)
                    for t in range(NT):
                        dve.wait_ge(s_acc, b.n * MT + c * NT + t + 1)
                        xs = xbuf[b.q][:, t, c * BANK:(c + 1) * BANK]
                        dve.tensor_tensor(xs, ps[:, ACC + t % 2, :], xs, ALU.add).then_inc(s_out, 1)
                        if f is not None:
                            slot(f, c * NT + t)
            batches(dve, step)

        @block.tensor
        def _(pe):
            pe.wait_ge(s_idn, 2)

            def flip(bank, at, src, n=P):
                return pe.transpose(ps[:, bank, at:at + n], src, ident[0:n, 0:n])

            def w_transposes(q, j):
                c, s = j // KC, j % KC
                for t in range(NT):
                    src = xbuf[q][:, t, c * BANK:(c + 1) * BANK].rearrange("p (m s) -> p s m", s=KC)[:, s, :]
                    ins = flip(j % RING, t * P, src)
                ins.then_inc(s_wt, 1)

            def w_products(q, g, j):
                n = g * KD + j
                pe.wait_ge(s_wlo, n + 1 + CREDIT)
                if j == 0:
                    pe.wait_ge(s_glo, g - 2 + 1 + 2)
                hi, lo = wT_r[:, j % RING, 0, :], wT_r[:, j % RING, 1, :]
                acc = ps[:, ACC + q, :]
                pe.matmul(acc, a_r[:, 0, j, :], hi, start=(j == 0), stop=False)
                pe.matmul(acc, a_r[:, 0, j, :], lo, start=False, stop=False)
                ins = pe.matmul(acc, a_r[:, 1, j, :], hi, start=False, stop=(j == KD - 1))
                ins.then_inc(s_wmm, 1)
                return ins

            LEAD = 3
            pe.wait_ge(s_alo, 1)
            with pe.Fori(0, W_GROUPS // 2) as i:
                for q in range(2):
                    g = i * 2 + q
                    for j in range(KD + LEAD):
                        if j < KD:
                            if j % KC == 0:
                                pe.wait_ge(s_load[q][j // KC], i * 16 + 16)
                            pe.wait_ge(s_wlo, g * KD + j - RING + 1 + CREDIT)
                            w_transposes(q, j)
                        if j >= LEAD:
                            w_products(q, g, j - LEAD)

            pe.wait_ge(s_condb, 16 * NB)
            pe.wait_ge(s_small, 48)
            pe.wait_ge(s_wlo, W_GROUPS * KD + CREDIT)
            by_s = [v.rearrange("p (c m s) -> p c s m", c=NC, s=KC) for v in (ffna_n, router_n[0:E, :])]
            for n in range(9):
                need(pe, s_se, n - RING + 1)
                if n < 4:
                    for j in range(4):
                        jj = 4 * n + j
                        ins = flip(n % RING, j * P, condb_n[:, jj * P:(jj + 1) * P])
                elif n < 8:
                    for j in range(4):
                        ins = flip(n % RING, j * P, by_s[0][:, n - 4, j, :])
                else:
                    for j in range(KD):
                        ins = flip(n % RING, j * E, by_s[1][:, j // KC, j % KC, :], E)
                ins.then_inc(s_st, 1)
            pe.wait_ge(s_se, 9)
            for j in range(KD):
                a_j = conda_n[:, :, j // KC, j % KC, :]
                ins = pe.matmul(ps[:, MISC, 0:P], ffnaT[:, j, :], a_j, start=(j == 0), stop=(j == KD - 1))
            ins.then_inc(s_sm, 1)
            for j in range(KD):
                a_j = conda_n[:, :, j // KC, j % KC, :]
                ins = pe.matmul(ps[0:E, BXB, 0:P], routerT[:, j, :], a_j, start=(j == 0), stop=(j == KD - 1))
            ins.then_inc(s_sm, 1)
            pe.wait_ge(s_grs, P // (2 * RK))
            pe.wait_ge(s_table, 2)
            for b in range(NB):
                ins = pe.matmul(ps[:, MISC, b * E:(b + 1) * E], grT[:, b].rearrange("e g u k -> e (g u k)"),
                                ident[0:E, 0:E], start=True, stop=True)
            ins.then_inc(s_sel, 1)
            for n in range(4 * NC * B_GROUPS):
                g, c, s = n // (4 * NC), n // 4 % NC, n % 4
                if s == 0:
                    pe.wait_ge(s_load[g][c], 16 * (W_GROUPS // 2 + NT))
                need(pe, s_be[n % 2], (n - RING) // 2 + 1)
                for t in range(NT):
                    ins = flip(n % RING, t * P, xbuf[g][:, t, c * BANK + s * P:c * BANK + (s + 1) * P])
                ins.then_inc(s_bt, 1)

            def h_products(b, c):
                pe.wait_ge(s_cur, b.n + 1)
                for h in range(2):
                    need(pe, s_hlo, (b.n * OC + c - 1) * 2 + h + 1)
                    for j in range(4):
                        ins = pe.matmul(ps[32 * j:32 * j + 32, HB + h, :], cur[:, b.q, TB_S:TB_S + 2 * RK],
                                        bexpT[:, 4 * h + j, c * BANK:(c + 1) * BANK], start=True, stop=True)
                    ins.then_inc(s_h, 1)

            def tile_products(b, c, t):
                m = c * NT + t
                acc = ps[:, ACC + t % 2, :]
                if m == 0:
                    pe.wait_ge(s_ulo, b.n * 2 + 2)
                    pe.wait_ge(s_sblo, b.n + 1)
                    pe.wait_ge(s_gm[b.q], b.half * 64 + 64)
                if t == 0:
                    pe.wait_ge(s_hlo, (b.n * OC + c) * 2 + 2)
                need(pe, s_out, b.n * MT + m - 1)
                tok_t = slice(t * P, (t + 1) * P)
                for h in range(2):
                    hi, lo = h_r[:, c % 2, 0, h, :], h_r[:, c % 2, 1, h, :]
                    pe.matmul(acc, u_r[:, b.q, 0, h, tok_t], hi, start=(h == 0), stop=False)
                    pe.matmul(acc, u_r[:, b.q, 0, h, tok_t], lo, start=False, stop=False)
                    pe.matmul(acc, u_r[:, b.q, 1, h, tok_t], hi, start=False, stop=False)
                pe.matmul(acc, sbx_r[:, b.q, tok_t], gm_r[:, b.q, c * BANK:(c + 1) * BANK], start=False, stop=True)\
                  .then_inc(s_acc, 1)

            def slot(f, m):
                if m in Q_AT:
                    c = Q_AT[m]
                    pe.wait_ge(s_xe, f.n * KD + 4 * c + 4)
                    if c == 0:
                        pe.wait_ge(s_cur, f.n + 1)
                        need(pe, s_up, f.n * 2)
                    for j in range(4):
                        jj = 4 * c + j
                        w = cur[:, f.q, jj * RK:(jj + 2) * RK]
                        ins = pe.matmul(ps[32 * j:32 * j + 32, BXB, :], w, xT[:, j, :],
                                        start=(c == 0), stop=(c == NC - 1))
                    ins.then_inc(s_bxq, 1)
                for j in T_AT.get(m, ()):
                    if j % 4 == 0:
                        pe.wait_ge(s_load[f.q][j // 4], load_count(f))
                    need(pe, s_xe, f.n * KD + j - 1)
                    for t in range(NT):
                        ins = flip(XP + j % 2, t * P, xbuf[f.q][:, t, j * P:(j + 1) * P])
                    ins.then_inc(s_xt, 1)
                if m == SPREAD_AT:
                    pe.wait_ge(s_bxp, f.n + 1)
                    for t in range(NT):
                        ins = pe.matmul(ps[:, MISC, t * E:(t + 1) * E], bxp[:, t * P:(t + 1) * P],
                                        cur[:, f.q, TB_R:TB_R + E], start=True, stop=True)
                    ins.then_inc(s_lg, 1)
                    pe.matmul(ps[:, BXB, :], spread[:, :], bxp,
                              start=True, stop=True).then_inc(s_rep, 1)
                if m in CT_AT:
                    h = CT_AT[m]
                    pe.wait_ge(s_combk, f.n * 2 + 2)
                    if h == 1:
                        pe.wait_ge(s_bx, f.n + 1)
                    for t in range(NT):
                        w = combk[:, t, h * EH:(h + 1) * EH, :].rearrange("p e k -> p (e k)")
                        ins = flip((MISC, BXB)[h], t * P, w)
                    ins.then_inc(s_ct, 1)

            def load_count(f):
                return f.half * 16 + 16 * (W_GROUPS // 2 + NT + 1)

            pe.wait_ge(s_be[0], 2 * NC * B_GROUPS)
            pe.wait_ge(s_be[1], 2 * NC * B_GROUPS)
            pe.wait_ge(s_glo, W_GROUPS + 2)
            pe.wait_ge(s_sum, 2)
            pe.wait_ge(s_biaslo, 2)
            first = Batch(0, 0)
            for m in range(MT):
                slot(first, m)
            h_products(first, 0)

            def step(b, f):
                for c in range(OC):
                    if c < OC - 1:
                        h_products(b, c + 1)
                    elif f is not None:
                        h_products(f, 0)
                    for t in range(NT):
                        tile_products(b, c, t)
                        if f is not None:
                            slot(f, c * NT + t)
            batches(pe, step)


_INS = ["x", "itok_B_3_7", "L0_cond_A", "L0_cond_B", "L0_ffn_base_w", "L0_ffn_base_b", "L0_ffn_A", "L0_ffn_B",
        "L0_ffn_router_w"]


def kernel(**inputs):
    import numpy as np
    import concourse.bacc as bacc
    from concourse.bass_utils import run_bass_kernel_spmd

    nc = bacc.Bacc("TRN2", target_bir_lowering=False, num_devices=1)
    arrays, args = {}, []
    for name in _INS:
        a = np.ascontiguousarray(inputs[name])
        arrays[f"in_{name}"] = a
        args.append(nc.dram_tensor(f"in_{name}", a.shape, mybir.dt.from_np(a.dtype), kind="ExternalInput").ap())
    shape = inputs["x"].shape
    args.append(nc.dram_tensor("out_0", shape, F32, kind="ExternalOutput").ap())
    adaln_ffn(nc, *args)
    r = run_bass_kernel_spmd(nc, [arrays], core_ids=[0])
    return r.results[0]["out_0"]
```

```python
from contextlib import ExitStack

import concourse.bass as bass
from concourse import mybir

F32 = mybir.dt.float32
F32R = mybir.dt.float32r
I32 = mybir.dt.int32
U32 = mybir.dt.uint32
ALU = mybir.AluOpType
ACT = mybir.ActivationFunctionType
AX = mybir.AxisListType

P = 128
BANK = 512
RING = 4


def adaln_ffn(nc, x, itok, cond_A, cond_B, base_w, base_b, ffn_A, ffn_B, router_w, out):
    NB, T, D = x.shape
    NAD, _, RK = cond_A.shape
    E, O, R = ffn_B.shape
    NT = T // P
    NC = D // BANK
    KD = D // P
    KC = KD // NC
    OC = O // BANK
    EH = E // 2
    NP = E // 2
    MT = OC * NT
    assert T == BANK and NB * RK == P and 2 * R == P and EH * RK == P and D == O
    W_GROUPS = O // (NT * P)
    B_GROUPS = 2
    X_GROUP0 = W_GROUPS + B_GROUPS
    TB_S, TB_R, TB = D // P * RK, D // P * RK + 2 * RK, D // P * RK + 3 * RK

    x_v = x.rearrange("b (t p) d -> b p t d", p=P)
    out_v = out.rearrange("b (t p) d -> b p t d", p=P)
    w_v = base_w.rearrange("(g t p) d -> g p t d", t=NT, p=P)
    bexp_v = ffn_B.rearrange("e (c p t) r -> c p e (t r)", t=NT, p=P)
    condA_v = cond_A.rearrange("n (c p s) k -> n p c (s k)", p=P, s=KC)

    with ExitStack() as ctx:
        def sb(name, shape, dt=F32):
            return ctx.enter_context(nc.sbuf_tensor(name, shape, dt))

        def sem(name):
            return ctx.enter_context(nc.semaphore(name))

        g_dram = nc.dram_tensor("g_hilo", (2, P, O), F32, kind="Internal").ap()

        xbuf = [sb(f"xbuf{q}", [P, NT, D]) for q in range(2)]
        bexpT = sb("bexpT", [P, NP, O])
        h_r = sb("h_r", [P, 2, 2, 2, BANK], F32R)
        u_r = sb("u_r", [P, 2, 2, 2, T], F32R)
        sbx_r = sb("sbx_r", [P, 2, T], F32R)
        gm_r = sb("gm_r", [P, 2, O], F32R)
        xT = sb("xT", [P, RING, T])
        table = sb("table", [P, NB, TB])
        cur = sb("cur", [P, 2, TB])
        tmp = sb("tmp", [P, 2, T])
        bxp = tmp[:, 0, :]
        bx = sb("bx", [P, T])
        ident = sb("ident", [P, P])
        spread = sb("spread", [P, P])
        iota_e = sb("iota_e", [P, E])
        tok = sb("tok", [1, NB], I32)
        mx = sb("mx", [P, NT])
        ex = sb("ex", [P, NT, E])
        ssum = sb("ssum", [P, NT])
        rs = sb("rs", [P, NT])
        top = sb("top", [P, NT, 8])
        sel = xT[:, 0, 0:NT * 2 * E].rearrange("p (t k e) -> p t k e", t=NT, k=2)
        comb = xT[:, 1, 0:NT * E].rearrange("p (t e) -> p t e", t=NT)
        wt2 = xT[:, 1, 128:128 + 2 * NT].rearrange("p (t k) -> p t k", t=NT)
        topf = xT[:, 1, 256:256 + 2 * NT].rearrange("p (t k) -> p t k", t=NT)
        topi = xT[:, 1, 384:384 + 8 * NT].bitcast(U32).rearrange("p (t k) -> p t k", t=NT)
        combk = xT[:, 2:4, :].rearrange("p a (t e k) -> p (a t) e k", e=E, k=RK)

        flat = bexpT[:, :, :].rearrange("p a o -> p (a o)")
        def carve(at, n):
            return flat[:, at:at + n]
        condb_n = carve(0, D)
        ffna_n = carve(D, D)[0:R + E, :]
        conda_n = carve(3 * D, D).rearrange("p (b c s k) -> p b c s k", b=NB, c=NC, s=KC)
        ffnaT = carve(4 * D, KD * (R + E)).rearrange("p (j m) -> p j m", j=KD)
        sum16 = carve(5 * D, RK)
        grT = carve(7 * D, NB * P)[0:E, :].rearrange("e (b g u k) -> e b g u k", b=NB, u=2, k=RK)
        bias_n = carve(6 * D, O)
        a_r = u_r[:, :, :, :, :].rearrange("p q l h t -> p (q l h t)").rearrange("p (l j m) -> p l j m", l=2, j=KD)
        wT_r = h_r[:, :, :, :, :].rearrange("p s l h o -> p (s l h) o").rearrange("p (n l) o -> p n l o", n=RING)

        ps = ctx.enter_context(nc.psum_tensor("ps", [P, 8, BANK], F32))
        XP, HB, ACC, MISC, BXB = 0, 2, 4, 6, 7

        s_const, s_idn, s_sum, s_iota = sem("const"), sem("idn"), sem("sum16"), sem("iota")
        s_tok, s_conda, s_condb, s_small, s_bias = sem("tok"), sem("conda"), sem("condb"), sem("small"), sem("bias")
        s_asked = sem("conda_asked")
        s_load = [[sem(f"load{q}{c}") for c in range(NC)] for q in range(2)]
        s_store = [sem(f"store{c}") for c in range(OC)]
        s_gst, s_gm = sem("g_stored"), [sem("gm0"), sem("gm1")]
        s_biashi, s_biaslo = sem("bias_hi"), sem("bias_lo")
        s_ahi, s_alo = sem("a_hi"), sem("a_lo")
        s_wt, s_whi, s_wlo, s_wmm = sem("w_transposed"), sem("w_hi"), sem("w_lo"), sem("w_used")
        s_ghi, s_glo = sem("g_hi"), sem("g_lo")
        s_st, s_se = sem("small_transposed"), sem("small_copied")
        s_sm, s_grs, s_sel, s_table = sem("ga_gr"), sem("gr_copied"), sem("gr_spread"), sem("table_done")
        s_bt, s_be = sem("b_transposed"), [sem("b_even"), sem("b_odd")]
        s_cur = sem("cur")
        s_xt, s_xe, s_bxq = sem("x_transposed"), sem("xT_copied"), sem("bx_quad")
        s_bxp, s_lg, s_rep, s_bx = sem("bx_partial"), sem("logits"), sem("bx_spread"), sem("bx_copied")
        s_lm, s_exp, s_comb, s_ct = sem("logits_minus_max"), sem("exp"), sem("comb"), sem("comb_transposed")
        s_combk = sem("comb_by_k")
        s_up, s_uhi, s_ulo = sem("u_product"), sem("u_hi"), sem("u_lo")
        s_sbhi, s_sblo = sem("sb_hi"), sem("sb_lo")
        s_h, s_hhi, s_hlo = sem("h_done"), sem("h_hi"), sem("h_lo")
        s_acc, s_out = sem("tile_done"), sem("tile_added")
        s_dve, s_gate = sem("dve_chain"), sem("dve_gate")
        CREDIT = RING
        DVE_PER_FRONT = 17

        def need(eng, s, v):
            if not isinstance(v, int) or v > 0:
                eng.wait_ge(s, v)

        def f32(ap):
            return ap.bitcast(F32)

        class Batch:
            def __init__(self, half, q):
                self.half, self.q, self.n = half, q, half * 2 + q

        def batches(eng, step):
            step(Batch(0, 0), Batch(0, 1))
            with eng.Fori(0, NB // 2 - 1) as i:
                step(Batch(i, 1), Batch(i + 1, 0))
                step(Batch(i + 1, 0), Batch(i + 1, 1))
            step(Batch(NB // 2 - 1, 1), None)

        B_RING = 4 * NC * B_GROUPS // 2
        B_AT = {m: (B_RING + m,) if m < 8 else (B_RING + 2 * m - 8, B_RING + 2 * m - 7) for m in range(12)}
        H_AT = 12

        def b_bank(n):
            return n % RING if n < B_RING else HB + n % 2

        def copy_b(eng, copy, n):
            g, c, s = n // (4 * NC), n // 4 % NC, n % 4
            oc, pair = 2 * g + c // 2, 4 * (c % 2) + s
            eng.wait_ge(s_bt, n + 1)
            bank = ps[:, b_bank(n), :].rearrange("p (e h m) -> p e h m", e=2, h=2)
            for e in range(2):
                dst = bexpT[e * R:(e + 1) * R, pair, oc * BANK:(oc + 1) * BANK]\
                    .rearrange("p (m h l) -> p l h m", h=2, l=2)
                for l in range(2):
                    ins = copy(dst[:, l], bank[l * R:(l + 1) * R, e])
            ins.then_inc(s_be[n % 2], 1)

        T_AT = {m: (2 * m, 2 * m + 1) for m in range(8)}
        Q_AT = {2: 0, 4: 1, 6: 2, 8: 3}
        SPREAD_AT, MAX_AT, EXP_AT, TOP_AT, COMB_AT, COMBK_AT = 9, 9, 9, 10, 11, 12
        CT_AT = UP_AT = {13: 0, 14: 1}
        LO_AT = {14: 0, 15: 1}

        block = ctx.enter_context(nc.Block())

        @block.sync
        def _(sp):
            def load_w(g, c):
                sp.dma_start(xbuf[g % 2][:, :, c * BANK:(c + 1) * BANK],
                             w_v[g, :, :, c * BANK:(c + 1) * BANK]).then_inc(s_load[g % 2][c], 16)

            def load_b(g, c):
                q, oh, eh = g % 2, c // 2, c % 2
                for s in range(NT):
                    e = eh * EH + 2 * s
                    dst = xbuf[q][:, s, c * BANK:(c + 1) * BANK].rearrange("p (e f) -> p e f", e=2)
                    sp.dma_start(dst, bexp_v[2 * (g - W_GROUPS) + oh, :, e:e + 2, :]).then_inc(s_load[q][c], 16)

            def load_x(b, q, c):
                sp.dma_start(xbuf[q][:, :, c * BANK:(c + 1) * BANK],
                             x_v[b, :, :, c * BANK:(c + 1) * BANK]).then_inc(s_load[q][c], 16)

            sp.dma_start(ffna_n[0:R, :], ffn_A).then_inc(s_small, 16)
            sp.dma_start(ffna_n[R:R + E, :], router_w).then_inc(s_small, 16)
            for row in (64, 96):
                sp.dma_start(bias_n[row:row + 1, :], base_b.rearrange("(a o) -> a o", a=1)).then_inc(s_bias, 16)
            for g in range(2):
                for c in range(NC):
                    if (g, c) == (0, 2):
                        sp.wait_ge(s_asked, 1)
                    load_w(g, c)
            def load_gm(b, q):
                for rep in range(2):
                    for l in range(2):
                        row = (2 * rep + l) * RK
                        sp.dma_start(f32(gm_r[row:row + RK, q, :]),
                                     g_dram[l, bass.ds(b * RK, RK), :]).then_inc(s_gm[q], 16)

            for g in range(2, X_GROUP0 + 2):
                if g == W_GROUPS:
                    sp.wait_ge(s_biaslo, 1)
                    sp.dma_start(f32(gm_r[64:P, 1, :]), f32(gm_r[64:P, 0, :])).then_inc(s_bias, 16)
                if g == X_GROUP0 + 1:
                    sp.wait_ge(s_gst, 16 * (W_GROUPS + 1))
                    load_gm(0, 0)
                for c in range(NC):
                    if g - 2 < W_GROUPS:
                        sp.wait_ge(s_wt, KD * (g - 2) + KC * (c + 1))
                    else:
                        sp.wait_ge(s_bt, 4 * NC * (g - 2 - W_GROUPS) + 4 * (c + 1))
                    if g < W_GROUPS:
                        load_w(g, c)
                    elif g < X_GROUP0:
                        load_b(g, c)
                    else:
                        load_x(g - X_GROUP0, g % 2, c)
                if g - 2 < W_GROUPS:
                    sp.wait_ge(s_glo, g - 2 + 1 + 2)
                    sp.dma_start(g_dram[:, :, (g - 2) * BANK:(g - 1) * BANK].rearrange("l p o -> p l o"),
                                 tmp[:, :, :]).then_inc(s_gst, 16)

            def step(b, f):
                if f is not None:
                    need(sp, s_acc, b.n * MT)
                    load_gm(f.n, f.q)
                for c in range(OC):
                    sp.wait_ge(s_out, b.n * MT + NT * (c + 1))
                    sp.dma_start(out_v[b.n, :, :, c * BANK:(c + 1) * BANK],
                                 xbuf[b.q][:, :, c * BANK:(c + 1) * BANK]).then_inc(s_store[c], 16)
                    if c > 0:
                        reload(b, c - 1)
                reload(b, OC - 1)

            def reload(b, c):
                if isinstance(b.n, int) and b.n + 2 >= NB:
                    return
                sp.wait_ge(s_store[c], b.n * 16 + 16)
                load_x(b.n + 2, b.q, c)

            step(Batch(0, 0), Batch(0, 1))
            with sp.Fori(0, NB // 2 - 2) as i:
                step(Batch(i, 1), Batch(i + 1, 0))
                step(Batch(i + 1, 0), Batch(i + 1, 1))
            h = NB // 2 - 2
            step(Batch(h, 1), Batch(h + 1, 0))
            step(Batch(h + 1, 0), Batch(h + 1, 1))
            step(Batch(h + 1, 1), None)
            for c in range(OC):
                sp.wait_ge(s_store[c], 16 * NB)

        @block.gpsimd
        def _(pool):
            pool.memset(ident[:, :], 0.0).then_inc(s_idn, 1)
            pool.wait_ge(s_idn, 1)
            pool.affine_select(out=ident[:, :], in_=ident[:, :], compare_op=ALU.not_equal, fill=1.0, base=0,
                               pattern=[[-1, P]], channel_multiplier=1).then_inc(s_idn, 1)
            pool.sem_inc(s_wlo, CREDIT)
            pool.sem_inc(s_wmm, CREDIT)
            pool.sem_inc(s_glo, 2)
            pool.sem_inc(s_gst, 16)
            fills = [(f32(gm_r[64:P, 0, :]), 0.0), (grT, 0.0), (table[:, :, :], 0.0), (f32(sbx_r[64:P, :, :]), 1.0)]
            pool.wait_ge(s_idn, 2)
            for n, (where, value) in enumerate(fills):
                pool.memset(where, value).then_inc(s_const, 1)
                pool.wait_ge(s_const, n + 1)
            pool.iota(iota_e[:, :], [[1, E]], base=0, channel_multiplier=0,
                      allow_small_or_imprecise_dtypes=True).then_inc(s_iota, 1)
            pool.wait_ge(s_iota, 1)

            pool.wait_ge(s_bias, 32)
            for n, row in enumerate((64, 96)):
                pool.tensor_copy(gm_r[row:row + 1, 0, :], bias_n[row:row + 1, :]).then_inc(s_biashi, 1)
                pool.wait_ge(s_biashi, n + 1)
            pool.tensor_tensor(gm_r[96:97, 0, :], bias_n[96:97, :], f32(gm_r[96:97, 0, :]), ALU.subtract)\
                .then_inc(s_biaslo, 1)

            def take(f):
                pool.wait_ge(s_se, 8)
                pool.wait_ge(s_table, 3)
                need(pool, s_h, (f.n - 1) * 2 * OC)
                need(pool, s_lg, f.n - 1)
                pool.tensor_copy(cur[:, f.q, :], table[:, f.n, :]).then_inc(s_cur, 1)

            take(Batch(0, 0))

            def step(b, f):
                if f is not None:
                    take(f)
            batches(pool, step)

        @block.scalar
        def _(act):
            def copy(dst, src):
                return act.activation(dst, src, ACT.Copy)

            def by_chunk(ap):
                return ap.rearrange("p b c s k -> p (c s) b k")

            act.dma_start(tok[:, :], itok.rearrange("(a b) -> a b", a=1)).then_inc(s_tok, 16)
            act.wait_ge(s_tok, 16)
            ids = []
            for b in range(NB):
                ids.append(act.value_load(tok[0:1, b:b + 1], min_val=0, max_val=NAD - 1))
                act.dma_start(conda_n[:, b, :, :, :].rearrange("p c s k -> p c (s k)"),
                              condA_v[ids[b], :, :, :]).then_inc(s_conda, 16)
            act.sem_inc(s_asked, 1)
            for b in range(NB):
                act.dma_start(condb_n[b * RK:(b + 1) * RK, :], cond_B[ids[b], :, :]).then_inc(s_condb, 16)
            act.wait_ge(s_conda, 16 * NB)
            copy(a_r[:, 0, :, :].rearrange("p j (b k) -> p j b k", b=NB), by_chunk(conda_n)).then_inc(s_ahi, 1)

            with act.Fori(0, W_GROUPS // 2) as i:
                for q in range(2):
                    g = i * 2 + q
                    for j in range(KD):
                        n = g * KD + j
                        act.wait_ge(s_wt, n + 1)
                        act.wait_ge(s_wmm, n - RING + 1 + CREDIT)
                        copy(wT_r[:, j % RING, 0, :], ps[:, j % RING, :]).then_inc(s_whi, 1)
                    act.wait_ge(s_wmm, (g + 1) * KD + CREDIT)
                    act.wait_ge(s_gst, g * 16 + 16)
                    copy(tmp[:, 0, :].bitcast(F32R), ps[:, ACC + q, :]).then_inc(s_ghi, 1)

            for n in range(0, B_RING, 2):
                copy_b(act, copy, n)

            def h_hi(b, c):
                for h in range(2):
                    act.wait_ge(s_h, (b.n * OC + c) * 2 + h + 1)
                    if h == 0:
                        need(act, s_acc, (b.n * OC + c - 1) * NT)
                    copy(h_r[:, c % 2, 0, h, :], ps[:, HB + h, :]).then_inc(s_hhi, 1)

            def slot(f, m):
                for j in T_AT.get(m, ()):
                    n = f.n * KD + j
                    act.wait_ge(s_xt, n + 1)
                    if j % 4 == 0:
                        need(act, s_bxq, f.n * NC + j // 4)
                    if j == 0:
                        need(act, s_ct, f.n * 2)
                    copy(xT[:, j % RING, :], ps[:, XP + j % 2, :]).then_inc(s_xe, 1)
                if m == 8:
                    act.wait_ge(s_bxq, f.n * NC + NC)
                    need(act, s_ulo, f.n * 2)
                    copy(bxp, ps[:, BXB, :]).then_inc(s_bxp, 1)
                if m == EXP_AT:
                    act.wait_ge(s_lm, f.n + 1)
                    act.activation(ex[:, :, :], ex[:, :, :], ACT.Exp).then_inc(s_exp, 1)
                if m == SPREAD_AT:
                    act.wait_ge(s_rep, f.n + 1)
                    need(act, s_up, f.n * 2)
                    copy(bx[:, :], ps[:, BXB, :]).then_inc(s_bx, 1)
                    act.wait_ge(s_bx, f.n + 1)
                    need(act, s_acc, (f.n - 1) * MT)
                    copy(sbx_r[0:64, f.q, :], bx[0:64, :]).then_inc(s_sbhi, 1)
                if m == COMBK_AT:
                    act.wait_ge(s_comb, f.n + 1)
                    for a in range(2):
                        copy(combk[:, 2 * a:2 * a + 2].rearrange("p t e k -> p (t e) k"),
                             comb[:, 2 * a:2 * a + 2].rearrange("p t e -> p (t e)").unsqueeze(2)
                             .to_broadcast([P, 2 * E, RK])).then_inc(s_combk, 1)
                if m in UP_AT:
                    h = UP_AT[m]
                    act.wait_ge(s_up, f.n * 2 + h + 1)
                    copy(u_r[:, f.q, 0, h, :], tmp[:, h, :]).then_inc(s_uhi, 1)

            act.wait_ge(s_gst, 16 * (W_GROUPS + 1))
            first = Batch(0, 0)
            for m in range(MT):
                slot(first, m)
                for n in B_AT.get(m, ()):
                    if n % 2 == 0:
                        copy_b(act, copy, n)
                if m == H_AT:
                    h_hi(first, 0)

            def step(b, f):
                for c in range(OC):
                    if c < OC - 1:
                        h_hi(b, c + 1)
                    elif f is not None:
                        h_hi(f, 0)
                    for t in range(NT):
                        if f is not None:
                            slot(f, c * NT + t)
            batches(act, step)

        @block.vector
        def _(dve):
            dve.wait_ge(s_idn, 2)
            dve.tensor_reduce(sum16, ident[:, :].rearrange("p (g u k) -> p u k g", u=2, k=RK)[:, 0], AX.X, ALU.add)\
               .then_inc(s_sum, 1)
            dve.wait_ge(s_sum, 1)
            dve.tensor_copy(spread[:, :].rearrange("p (g k) -> p g k", k=RK),
                            sum16.unsqueeze(1).to_broadcast([P, P // RK, RK])).then_inc(s_sum, 1)
            tb = table[:, :, 0:KD * RK].rearrange("p b (j k) -> p j b k", k=RK)

            def small_copy(n):
                dve.wait_ge(s_st, n + 1)
                bank = ps[:, n % RING, :]
                if n < 4:
                    dst, src = ffnaT[:, 4 * n:4 * n + 4, :], bank.rearrange("p (j m) -> p j m", j=4)[:, :, 0:R + E]
                else:
                    dst, src = tb[:, 4 * (n - 4):4 * (n - 3)], bank.rearrange("p (j b k) -> p j b k", j=4, b=NB)
                dve.tensor_copy(dst, src).then_inc(s_se, 1)

            for n in range(4):
                small_copy(n)
            dve.wait_ge(s_ahi, 1)
            by_b = a_r[:, :, :, :].rearrange("p l j (b k) -> p l j b k", b=NB)
            dve.tensor_tensor(by_b[:, 1], conda_n.rearrange("p b c s k -> p (c s) b k"), f32(by_b[:, 0]),
                              ALU.subtract).then_inc(s_alo, 1)
            dve.wait_ge(s_const, 4)
            dve.wait_ge(s_sm, 1)
            ga = ps[:, MISC, 0:P].rearrange("p (b k) -> p b k", b=NB)
            for n in range(2):
                dve.tensor_scalar(table[n * R:(n + 1) * R, :, TB_S + n * RK:TB_S + (n + 1) * RK],
                                  ga[0:R], 0.5, None, ALU.mult).then_inc(s_table, 1)
            for g in range(P // (2 * RK)):
                dve.tensor_copy(grT[:, :, g, 0, :], ps[R:R + E, MISC, 0:P].rearrange("p (b k) -> p b k", b=NB))\
                   .then_inc(s_grs, 1)

            with dve.Fori(0, W_GROUPS // 2) as i:
                for q in range(2):
                    g = i * 2 + q
                    for j in range(KD):
                        n = g * KD + j
                        dve.wait_ge(s_whi, n + 1)
                        dve.tensor_tensor(wT_r[:, j % RING, 1, :], ps[:, j % RING, :],
                                          f32(wT_r[:, j % RING, 0, :]), ALU.subtract).then_inc(s_wlo, 1)
                    dve.wait_ge(s_ghi, g + 1)
                    dve.tensor_tensor(tmp[:, 1, :].bitcast(F32R), ps[:, ACC + q, :], tmp[:, 0, :], ALU.subtract)\
                       .then_inc(s_glo, 1)

            for n in range(4, 8):
                small_copy(n)
            dve.wait_ge(s_sel, 1)
            dve.tensor_copy(table[:, :, TB_R:TB_R + E], ps[:, BXB, 0:NB * E].rearrange("p (b e) -> p b e", b=NB))\
               .then_inc(s_table, 1)

            for n in range(1, B_RING, 2):
                copy_b(dve, dve.tensor_copy, n)

            def h_lo(b, c):
                for h in range(2):
                    dve.wait_ge(s_hhi, (b.n * OC + c) * 2 + h + 1)
                    dve.tensor_tensor(h_r[:, c % 2, 1, h, :], ps[:, HB + h, :], f32(h_r[:, c % 2, 0, h, :]),
                                      ALU.subtract).then_inc(s_hlo, 1)

            def slot(f, m):
                base = f.n * DVE_PER_FRONT
                at = {MAX_AT: 0, TOP_AT: 1, COMB_AT: 10}.get(m, 0)
                count = [at]

                def link(ins):
                    count[0] += 1
                    return ins.then_inc(s_dve, 1)

                def after(n=None):
                    dve.wait_ge(s_dve, base + (count[0] if n is None else n))

                def wide(ap):
                    return ap.unsqueeze(2).to_broadcast([P, NT, E])

                if m == MAX_AT:
                    dve.wait_ge(s_lg, f.n + 1)
                    lg = ps[:, MISC, 0:NT * E].rearrange("p (t e) -> p t e", t=NT)
                    link(dve.tensor_reduce(mx[:, :], lg, AX.X, ALU.max))
                    after()
                    dve.tensor_tensor(ex[:, :, :], lg, wide(mx[:, :]), ALU.subtract).then_inc(s_lm, 1)
                if m == TOP_AT:
                    dve.wait_ge(s_exp, f.n + 1)
                    link(dve.tensor_reduce(ssum[:, :], ex[:, :, :], AX.X, ALU.add))
                    after()
                    link(dve.reciprocal(rs[:, :], ssum[:, :]))
                    after()
                    link(dve.tensor_tensor(ex[:, :, :], ex[:, :, :], wide(rs[:, :]), ALU.mult))
                    after()
                    dve.sem_inc(s_gate, 1)
                    for t in range(NT):
                        link(dve.max(top[:, t, :], ex[:, t, :]))
                    after()
                    dve.sem_inc(s_gate, 1)
                    for t in range(NT):
                        ins = dve.max_index(topi[:, t, :], top[:, t, :], ex[:, t, :])
                        if t == NT - 1:
                            link(ins)
                    link(dve.scalar_tensor_tensor(out=rs[:, :], in0=top[:, :, 0], scalar=1e-6, in1=top[:, :, 1],
                                                  op0=ALU.add, op1=ALU.add))
                if m == COMB_AT:
                    after()
                    link(dve.reciprocal(ssum[:, :], rs[:, :]))
                    link(dve.tensor_copy(topf[:, :, :], topi[:, :, 0:2]))
                    after()
                    link(dve.tensor_tensor(wt2[:, :, :], top[:, :, 0:2],
                                           ssum[:, :].unsqueeze(2).to_broadcast([P, NT, 2]), ALU.mult))
                    iota_w = iota_e[:, :].unsqueeze(1).to_broadcast([P, NT, E])
                    for k in range(2):
                        link(dve.tensor_tensor(sel[:, :, k, :], iota_w, wide(topf[:, :, k]), ALU.is_equal))
                    after()
                    for k in range(2):
                        link(dve.tensor_tensor(sel[:, :, k, :], sel[:, :, k, :], wide(wt2[:, :, k]), ALU.mult))
                    after()
                    dve.tensor_tensor(comb[:, :, :], sel[:, :, 0, :], sel[:, :, 1, :], ALU.add).then_inc(s_comb, 1)
                if m == COMBK_AT:
                    dve.wait_ge(s_sbhi, f.n + 1)
                    dve.tensor_tensor(sbx_r[32:64, f.q, :], bx[32:64, :], f32(sbx_r[32:64, f.q, :]), ALU.subtract)\
                       .then_inc(s_sblo, 1)
                if m in UP_AT:
                    h = UP_AT[m]
                    dve.wait_ge(s_ct, f.n * 2 + h + 1)
                    need(dve, s_uhi, f.n * 2 - 2 + h + 1)
                    dve.tensor_tensor(tmp[:, h, :], ps[:, (MISC, BXB)[h], :], bx[:, :], ALU.mult).then_inc(s_up, 1)
                if m in LO_AT:
                    for h in (LO_AT[m],):
                        dve.wait_ge(s_uhi, f.n * 2 + h + 1)
                        dve.tensor_tensor(u_r[:, f.q, 1, h, :], tmp[:, h, :], f32(u_r[:, f.q, 0, h, :]),
                                          ALU.subtract).then_inc(s_ulo, 1)

            first = Batch(0, 0)
            for m in range(MT):
                slot(first, m)
                for n in B_AT.get(m, ()):
                    if n % 2 == 1:
                        copy_b(dve, dve.tensor_copy, n)
                if m == H_AT:
                    h_lo(first, 0)

            def step(b, f):
                for c in range(OC):
                    if c < OC - 1:
                        h_lo(b, c + 1)
                    elif f is not None:
                        h_lo(f, 0)
                    for t in range(NT):
                        m = c * NT + t
                        if f is not None and m == MT - 1:
                            slot(f, m)
                        dve.wait_ge(s_acc, b.n * MT + m + 1)
                        xs = xbuf[b.q][:, t, c * BANK:(c + 1) * BANK]
                        dve.tensor_tensor(xs, ps[:, ACC + t % 2, :], xs, ALU.add).then_inc(s_out, 1)
                        if f is not None and m < MT - 1:
                            slot(f, m)
            batches(dve, step)

        @block.tensor
        def _(pe):
            pe.wait_ge(s_idn, 2)

            def flip(bank, at, src, n=P):
                return pe.transpose(ps[:, bank, at:at + n], src, ident[0:n, 0:n])

            def w_transposes(q, j):
                c, s = j // KC, j % KC
                for t in range(NT):
                    src = xbuf[q][:, t, c * BANK:(c + 1) * BANK].rearrange("p (m s) -> p s m", s=KC)[:, s, :]
                    ins = flip(j % RING, t * P, src)
                ins.then_inc(s_wt, 1)

            def w_products(q, g, j):
                n = g * KD + j
                pe.wait_ge(s_wlo, n + 1 + CREDIT)
                if j == 0:
                    pe.wait_ge(s_alo, 1)
                    pe.wait_ge(s_glo, g - 2 + 1 + 2)
                hi, lo = wT_r[:, j % RING, 0, :], wT_r[:, j % RING, 1, :]
                acc = ps[:, ACC + q, :]
                pe.matmul(acc, a_r[:, 0, j, :], hi, start=(j == 0), stop=False)
                pe.matmul(acc, a_r[:, 0, j, :], lo, start=False, stop=False)
                ins = pe.matmul(acc, a_r[:, 1, j, :], hi, start=False, stop=(j == KD - 1))
                ins.then_inc(s_wmm, 1)
                return ins

            pe.wait_ge(s_small, 32)
            by_s = ffna_n.rearrange("p (c m s) -> p c s m", c=NC, s=KC)
            for n in range(4):
                for j in range(4):
                    ins = flip(n, j * P, by_s[:, n, j, :], R + E)
                ins.then_inc(s_st, 1)
            pe.wait_ge(s_se, 4)
            pe.wait_ge(s_conda, 16 * NB)
            for j in range(KD):
                a_j = conda_n[:, :, j // KC, j % KC, :]
                ins = pe.matmul(ps[0:R + E, MISC, 0:P], ffnaT[:, j, :], a_j, start=(j == 0), stop=(j == KD - 1))
            ins.then_inc(s_sm, 1)

            LEAD = 3
            with pe.Fori(0, W_GROUPS // 2) as i:
                for q in range(2):
                    g = i * 2 + q
                    for j in range(KD + LEAD):
                        if j < KD:
                            if j % KC == 0:
                                pe.wait_ge(s_load[q][j // KC], i * 16 + 16)
                            pe.wait_ge(s_wlo, g * KD + j - RING + 1 + CREDIT)
                            w_transposes(q, j)
                        if j >= LEAD:
                            w_products(q, g, j - LEAD)

            pe.wait_ge(s_condb, 16 * NB)
            for n in range(4, 8):
                pe.wait_ge(s_wlo, W_GROUPS * KD + CREDIT)
                for j in range(4):
                    jj = 4 * (n - 4) + j
                    ins = flip(n % RING, j * P, condb_n[:, jj * P:(jj + 1) * P])
                ins.then_inc(s_st, 1)
            pe.wait_ge(s_grs, P // (2 * RK))
            for b in range(NB):
                ins = pe.matmul(ps[:, BXB, b * E:(b + 1) * E], grT[:, b].rearrange("e g u k -> e (g u k)"),
                                ident[0:E, 0:E], start=True, stop=True)
            ins.then_inc(s_sel, 1)
            def b_transposes(n):
                g, c, s = n // (4 * NC), n // 4 % NC, n % 4
                if s == 0:
                    pe.wait_ge(s_load[g][c], 16 * (W_GROUPS // 2 + NT))
                need(pe, s_be[n % 2], (n - (RING if n < B_RING else 2)) // 2 + 1)
                for u in range(4):
                    ins = flip(b_bank(n), u * P, xbuf[g][:, s, c * BANK + u * P:c * BANK + (u + 1) * P])
                ins.then_inc(s_bt, 1)

            pe.wait_ge(s_se, 8)
            for n in range(B_RING):
                b_transposes(n)

            def h_products(b, c):
                pe.wait_ge(s_cur, b.n + 1)
                for h in range(2):
                    need(pe, s_hlo, (b.n * OC + c - 1) * 2 + h + 1)
                    for j in range(4):
                        ins = pe.matmul(ps[32 * j:32 * j + 32, HB + h, :], cur[:, b.q, TB_S:TB_S + 2 * RK],
                                        bexpT[:, 4 * h + j, c * BANK:(c + 1) * BANK], start=True, stop=True)
                    ins.then_inc(s_h, 1)

            def tile_products(b, c, t):
                m = c * NT + t
                acc = ps[:, ACC + t % 2, :]
                if m == 0:
                    pe.wait_ge(s_ulo, b.n * 2 + 2)
                    pe.wait_ge(s_sblo, b.n + 1)
                    pe.wait_ge(s_gm[b.q], b.half * 64 + 64)
                if t == 0:
                    pe.wait_ge(s_hlo, (b.n * OC + c) * 2 + 2)
                need(pe, s_out, b.n * MT + m - 1)
                tok_t = slice(t * P, (t + 1) * P)
                for h in range(2):
                    hi, lo = h_r[:, c % 2, 0, h, :], h_r[:, c % 2, 1, h, :]
                    pe.matmul(acc, u_r[:, b.q, 0, h, tok_t], hi, start=(h == 0), stop=False)
                    pe.matmul(acc, u_r[:, b.q, 0, h, tok_t], lo, start=False, stop=False)
                    pe.matmul(acc, u_r[:, b.q, 1, h, tok_t], hi, start=False, stop=False)
                pe.matmul(acc, sbx_r[:, b.q, tok_t], gm_r[:, b.q, c * BANK:(c + 1) * BANK], start=False, stop=True)\
                  .then_inc(s_acc, 1)

            def slot(f, m):
                if m in Q_AT:
                    c = Q_AT[m]
                    pe.wait_ge(s_xe, f.n * KD + 4 * c + 4)
                    if c == 0:
                        pe.wait_ge(s_cur, f.n + 1)
                        need(pe, s_up, f.n * 2)
                    for j in range(4):
                        jj = 4 * c + j
                        w = cur[:, f.q, jj * RK:(jj + 2) * RK]
                        ins = pe.matmul(ps[32 * j:32 * j + 32, BXB, :], w, xT[:, j, :],
                                        start=(c == 0), stop=(c == NC - 1))
                    ins.then_inc(s_bxq, 1)
                for j in T_AT.get(m, ()):
                    if j % 4 == 0:
                        pe.wait_ge(s_load[f.q][j // 4], load_count(f))
                    need(pe, s_xe, f.n * KD + j - 1)
                    for t in range(NT):
                        ins = flip(XP + j % 2, t * P, xbuf[f.q][:, t, j * P:(j + 1) * P])
                    ins.then_inc(s_xt, 1)
                if m == SPREAD_AT:
                    pe.wait_ge(s_bxp, f.n + 1)
                    for t in range(NT):
                        ins = pe.matmul(ps[:, MISC, t * E:(t + 1) * E], bxp[:, t * P:(t + 1) * P],
                                        cur[:, f.q, TB_R:TB_R + E], start=True, stop=True)
                    ins.then_inc(s_lg, 1)
                    pe.matmul(ps[:, BXB, :], spread[:, :], bxp,
                              start=True, stop=True).then_inc(s_rep, 1)
                if m in CT_AT:
                    h = CT_AT[m]
                    pe.wait_ge(s_combk, f.n * 2 + 2)
                    if h == 1:
                        pe.wait_ge(s_bx, f.n + 1)
                    for t in range(NT):
                        w = combk[:, t, h * EH:(h + 1) * EH, :].rearrange("p e k -> p (e k)")
                        ins = flip((MISC, BXB)[h], t * P, w)
                    ins.then_inc(s_ct, 1)

            def load_count(f):
                return f.half * 16 + 16 * (W_GROUPS // 2 + NT + 1)

            for s in s_be:
                pe.wait_ge(s, B_RING // 2)
            pe.wait_ge(s_glo, W_GROUPS + 2)
            pe.wait_ge(s_sum, 2)
            pe.wait_ge(s_bias, 48)
            first = Batch(0, 0)
            for m in range(MT):
                slot(first, m)
                for n in B_AT.get(m, ()):
                    b_transposes(n)
                if m == H_AT:
                    for s in s_be:
                        pe.wait_ge(s, 2 * NC * B_GROUPS)
                    h_products(first, 0)

            def step(b, f):
                for c in range(OC):
                    if c < OC - 1:
                        h_products(b, c + 1)
                    elif f is not None:
                        h_products(f, 0)
                    for t in range(NT):
                        tile_products(b, c, t)
                        if f is not None:
                            slot(f, c * NT + t)
            batches(pe, step)


_INS = ["x", "itok_B_3_7", "L0_cond_A", "L0_cond_B", "L0_ffn_base_w", "L0_ffn_base_b", "L0_ffn_A", "L0_ffn_B",
        "L0_ffn_router_w"]


def kernel(**inputs):
    import numpy as np
    import concourse.bacc as bacc
    from concourse.bass_utils import run_bass_kernel_spmd

    nc = bacc.Bacc("TRN2", target_bir_lowering=False, num_devices=1)
    arrays, args = {}, []
    for name in _INS:
        a = np.ascontiguousarray(inputs[name])
        arrays[f"in_{name}"] = a
        args.append(nc.dram_tensor(f"in_{name}", a.shape, mybir.dt.from_np(a.dtype), kind="ExternalInput").ap())
    shape = inputs["x"].shape
    args.append(nc.dram_tensor("out_0", shape, F32, kind="ExternalOutput").ap())
    adaln_ffn(nc, *args)
    r = run_bass_kernel_spmd(nc, [arrays], core_ids=[0])
    return r.results[0]["out_0"]
```

```python
from contextlib import ExitStack

import concourse.bass as bass
from concourse import mybir

F32 = mybir.dt.float32
F32R = mybir.dt.float32r
I32 = mybir.dt.int32
U32 = mybir.dt.uint32
ALU = mybir.AluOpType
ACT = mybir.ActivationFunctionType
AX = mybir.AxisListType

P = 128
BANK = 512
RING = 4


def adaln_ffn(nc, x, itok, cond_A, cond_B, base_w, base_b, ffn_A, ffn_B, router_w, out):
    NB, T, D = x.shape
    NAD, _, RK = cond_A.shape
    E, O, R = ffn_B.shape
    NT = T // P
    NC = D // BANK
    KD = D // P
    KC = KD // NC
    KS = KD // 2
    OC = O // BANK
    EH = E // 2
    NP = E // 2
    MT = OC * NT
    assert T == BANK and NB * RK == P and 2 * R == P and EH * RK == P and D == O
    W_GROUPS = O // (NT * P)
    B_GROUPS = 2
    X_GROUP0 = W_GROUPS + B_GROUPS
    TB_R, TB = 2 * RK, 3 * RK
    SQ = 32
    NQ = P // SQ

    x_v = x.rearrange("b (t p) d -> b p t d", p=P)
    out_v = out.rearrange("b (t p) d -> b p t d", p=P)
    w_v = base_w.rearrange("(g t p) d -> g p t d", t=NT, p=P)
    bexp_v = ffn_B.rearrange("e (c p t) r -> c p e (t r)", t=NT, p=P)
    condA_v = cond_A.rearrange("n (c p s) k -> n p c (s k)", p=P, s=KS)

    with ExitStack() as ctx:
        def sb(name, shape, dt=F32):
            return ctx.enter_context(nc.sbuf_tensor(name, shape, dt))

        def sem(name):
            return ctx.enter_context(nc.semaphore(name))

        g_dram = nc.dram_tensor("g_hilo", (2, P, O), F32, kind="Internal").ap()

        b_dram = nc.dram_tensor("b_t", (NB * NC, SQ, NQ, KC * RK), F32, kind="Internal").ap()

        xbuf = [sb(f"xbuf{q}", [P, NT, D]) for q in range(2)]
        bexpT = sb("bexpT", [P, NP, O])
        h_r = sb("h_r", [P, 2, 2, 2, BANK], F32R)
        u_r = sb("u_r", [P, 2, 2, 2, T], F32R)
        sbx_r = sb("sbx_r", [P, 2, T], F32R)
        gm_r = sb("gm_r", [P, 2, O], F32R)
        xT = sb("xT", [P, RING, T])
        bsrc = sb("bsrc", [P, 2, NQ * KC * RK])
        bdiag = sb("bdiag", [P, 2, NQ * KC, NQ * RK])
        in_square = sb("in_square", [P, NQ])
        in_block = sb("in_block", [P, NQ])
        table = sb("table", [P, NB, TB])
        cur = sb("cur", [P, 2, TB])
        tmp = sb("tmp", [P, 2, T])
        bxp = tmp[:, 0, :]
        bx = sb("bx", [P, T])
        ident = sb("ident", [P, P])
        spread = sb("spread", [P, P])
        iota_e = sb("iota_e", [P, E])
        tok = sb("tok", [1, NB], I32)
        mx = sb("mx", [P, NT])
        ex = sb("ex", [P, NT, E])
        ssum = sb("ssum", [P, NT])
        rs = sb("rs", [P, NT])
        top = sb("top", [P, NT, 8])
        sel = xT[:, 0, 0:NT * 2 * E].rearrange("p (t k e) -> p t k e", t=NT, k=2)
        comb = xT[:, 1, 0:NT * E].rearrange("p (t e) -> p t e", t=NT)
        wt2 = xT[:, 1, 128:128 + 2 * NT].rearrange("p (t k) -> p t k", t=NT)
        topf = xT[:, 1, 256:256 + 2 * NT].rearrange("p (t k) -> p t k", t=NT)
        topi = xT[:, 1, 384:384 + 8 * NT].bitcast(U32).rearrange("p (t k) -> p t k", t=NT)
        combk = xT[:, 2:4, :].rearrange("p a (t e k) -> p (a t) e k", e=E, k=RK)

        flat = bexpT[:, :, :].rearrange("p a o -> p (a o)")
        def carve(at, n):
            return flat[:, at:at + n]
        condb_n = carve(0, D)
        ffna_n = carve(D, D)[0:R + E, :]
        conda_n = carve(3 * D, D).rearrange("p (b c s k) -> p b c s k", b=NB, c=2, s=KS)
        ffnaT = carve(4 * D, KD * (R + E)).rearrange("p (j m) -> p j m", j=KD)
        sum16 = carve(5 * D, RK)
        sum8 = carve(5 * D + RK, P // RK)
        bias_n = carve(6 * D, O)
        bT = xT[:, :, :].rearrange("p a t -> p (a t)").rearrange("p (b j k) -> p j b k", b=NB, k=RK)
        grT = xT[0:E, 0:NB * P // T, :].rearrange("e a t -> e (a t)").rearrange("e (b g k) -> e b g k", b=NB, k=RK)
        a_r = u_r[:, :, :, :, :].rearrange("p q l h t -> p (q l h t)").rearrange("p (l j m) -> p l j m", l=2, j=KD)
        wT_r = h_r[:, :, :, :, :].rearrange("p s l h o -> p (s l h) o").rearrange("p (n l) o -> p n l o", n=RING)

        ps = ctx.enter_context(nc.psum_tensor("ps", [P, 8, BANK], F32))
        HB, ACC, MISC, BXB = 2, 4, 6, 7

        s_const, s_idn, s_masks, s_iota = sem("const"), sem("idn"), sem("masks"), sem("iota")
        s_tok, s_conda, s_condb, s_small, s_bias = sem("tok"), sem("conda"), sem("condb"), sem("small"), sem("bias")
        s_load = [[sem(f"load{q}{c}") for c in range(NC)] for q in range(2)]
        s_store = [sem(f"store{c}") for c in range(OC)]
        s_gst, s_gm = sem("g_stored"), [sem("gm0"), sem("gm1")]
        s_asked = sem("adapters_asked")
        s_biashi, s_biaslo = sem("bias_hi"), sem("bias_lo")
        s_ahi, s_alo = sem("a_hi"), sem("a_lo")
        s_wt, s_whi, s_wlo, s_wmm = sem("w_transposed"), sem("w_hi"), sem("w_lo"), sem("w_used")
        s_ghi, s_glo = sem("g_hi"), sem("g_lo")
        s_st, s_se = sem("small_transposed"), sem("small_copied")
        s_sm, s_grs, s_sel, s_table = sem("ga_gr"), sem("gr_copied"), sem("gr_spread"), sem("table_done")
        s_bt, s_b_act, s_b_dve = sem("b_transposed"), sem("b_by_act"), sem("b_by_dve")
        s_cur = sem("cur")
        s_bst, s_bsrc, s_bd = sem("bT_stored"), [sem("bsrc0"), sem("bsrc1")], sem("bdiag")
        s_xe, s_bxq = sem("x_transposed"), sem("bx_products")
        s_bxp, s_lg, s_rep, s_bx = sem("bx_partial"), sem("logits"), sem("bx_spread"), sem("bx_copied")
        s_lm, s_exp, s_comb, s_ct = sem("logits_minus_max"), sem("exp"), sem("comb"), sem("comb_transposed")
        s_combk = sem("comb_by_k")
        s_up, s_uhi, s_ulo = sem("u_product"), sem("u_hi"), sem("u_lo")
        s_sbhi, s_sblo = sem("sb_hi"), sem("sb_lo")
        s_h, s_hhi, s_hlo = sem("h_done"), sem("h_hi"), sem("h_lo")
        s_acc, s_out = sem("tile_done"), sem("tile_added")
        s_dve, s_gate = sem("dve_chain"), sem("dve_gate")
        CREDIT = RING
        DVE_PER_FRONT = 17

        def need(eng, s, v):
            if not isinstance(v, int) or v > 0:
                eng.wait_ge(s, v)

        def f32(ap):
            return ap.bitcast(F32)

        def h_is_there(b, c):
            return isinstance(b.n, int) and (b.n, c) == (0, 1)

        class Batch:
            def __init__(self, half, q):
                self.half, self.q, self.n = half, q, half * 2 + q

        def batches(eng, step):
            step(Batch(0, 0), Batch(0, 1))
            with eng.Fori(0, NB // 2 - 1) as i:
                step(Batch(i, 1), Batch(i + 1, 0))
                step(Batch(i + 1, 0), Batch(i + 1, 1))
            step(Batch(NB // 2 - 1, 1), None)

        B_RING = 4 * NC * B_GROUPS // 2
        B_MANY = (1, 1, 0, 1, 0, 1, 0, 1, 2, 2, 2, 2, 2, 1)
        B_AT, n = {}, B_RING
        for m, many in enumerate(B_MANY):
            B_AT[m] = range(n, n + many)
            n += many
        B_BY = "aadadadadadadaaa" "aaaaaadaadaadaad"
        H_AT = {11: 0, 15: 1}
        GR_AFTER = 7

        def small_bank(n):
            return n if n < 4 else (ACC + 1, BXB)[n % 2]

        def b_bank(n):
            return n % RING if n < B_RING else (0, 1, ACC, ACC + 1)[n % 4]

        def b_copied(eng, n):
            who = B_BY[n]
            eng.wait_ge(s_b_act if who == "a" else s_b_dve, B_BY[:n + 1].count(who))

        def copy_b(eng, copy, n):
            g, c, s = n // (4 * NC), n // 4 % NC, n % 4
            oc, pair = 2 * g + c // 2, 4 * (c % 2) + s
            eng.wait_ge(s_bt, n + 1)
            bank = ps[:, b_bank(n), :].rearrange("p (e h m) -> p e h m", e=2, h=2)
            for e in range(2):
                dst = bexpT[e * R:(e + 1) * R, pair, oc * BANK:(oc + 1) * BANK]\
                    .rearrange("p (m h l) -> p l h m", h=2, l=2)
                for l in range(2):
                    ins = copy(dst[:, l], bank[l * R:(l + 1) * R, e])
            ins.then_inc(s_b_act if B_BY[n] == "a" else s_b_dve, 1)

        T_AT = {m: (2 * m, 2 * m + 1) for m in range(8)}
        Q_AT = {m + 1: js for m, js in T_AT.items()}
        BXP_AT = 8
        SPREAD_AT, MAX_AT, EXP_AT, TOP_AT, COMB_AT, COMBK_AT = 9, 9, 9, 10, 11, 12
        CT_AT = UP_AT = {13: 0, 14: 1}
        LO_AT = {14: 0, 15: 1}

        def load_count(f):
            return f.half * 16 + 16 * (W_GROUPS // 2 + NT + 1)

        def load_adapters(eng, half):
            ids = {}
            for b in range(half, NB, 2):
                ids[b] = eng.value_load(tok[0:1, b:b + 1], min_val=0, max_val=NAD - 1)
                eng.dma_start(conda_n[:, b, :, :, :].rearrange("p c s k -> p c (s k)"),
                              condA_v[ids[b], :, :, :]).then_inc(s_conda, 16)
            for b in range(half, NB, 2):
                eng.dma_start(condb_n[b * RK:(b + 1) * RK, :], cond_B[ids[b], :, :]).then_inc(s_condb, 16)

        block = ctx.enter_context(nc.Block())

        @block.sync
        def _(sp):
            def load_w(g, c):
                sp.dma_start(xbuf[g % 2][:, :, c * BANK:(c + 1) * BANK],
                             w_v[g, :, :, c * BANK:(c + 1) * BANK]).then_inc(s_load[g % 2][c], 16)

            def load_b(g, c):
                q, oh, eh = g % 2, c // 2, c % 2
                for s in range(NT):
                    e = eh * EH + 2 * s
                    dst = xbuf[q][:, s, c * BANK:(c + 1) * BANK].rearrange("p (e f) -> p e f", e=2)
                    sp.dma_start(dst, bexp_v[2 * (g - W_GROUPS) + oh, :, e:e + 2, :]).then_inc(s_load[q][c], 16)

            def load_x(b, q, c):
                sp.dma_start(xbuf[q][:, :, c * BANK:(c + 1) * BANK],
                             x_v[b, :, :, c * BANK:(c + 1) * BANK]).then_inc(s_load[q][c], 16)

            sp.dma_start(ffna_n[0:R, :], ffn_A).then_inc(s_small, 16)
            sp.dma_start(ffna_n[R:R + E, :], router_w).then_inc(s_small, 16)
            for row in (64, 96):
                sp.dma_start(bias_n[row:row + 1, :], base_b.rearrange("(a o) -> a o", a=1)).then_inc(s_bias, 16)
            for g in range(2):
                for c in range(NC):
                    if (g, c) == (0, 1):
                        sp.wait_ge(s_tok, 16)
                        load_adapters(sp, 1)
                        sp.wait_ge(s_asked, 1)
                    load_w(g, c)

            def load_gm(b, q):
                for rep in range(2):
                    for l in range(2):
                        row = (2 * rep + l) * RK
                        sp.dma_start(f32(gm_r[row:row + RK, q, :]),
                                     g_dram[l, bass.ds(b * RK, RK), :]).then_inc(s_gm[q], 16)

            def load_bsrc(b, c):
                need(sp, s_bd, b * NC + c - 1)
                for tb in range(NQ):
                    sp.dma_start(bsrc[tb * SQ:(tb + 1) * SQ, c % 2, :],
                                 b_dram[bass.ds(b * NC + c, 1)].rearrange("a p q f -> p (a q f)"))\
                      .then_inc(s_bsrc[c % 2], 16)

            for g in range(2, X_GROUP0 + 2):
                if g == W_GROUPS:
                    sp.wait_ge(s_biaslo, 1)
                    sp.dma_start(f32(gm_r[64:P, 1, :]), f32(gm_r[64:P, 0, :])).then_inc(s_bias, 16)
                if g == X_GROUP0 + 1:
                    sp.wait_ge(s_gst, 16 * (W_GROUPS + 1))
                    load_gm(0, 0)
                if g == 2:
                    sp.wait_ge(s_se, 8)
                    for q in range(NQ):
                        sp.dma_start(b_dram[:, :, q, :].rearrange("n p f -> p n f"),
                                     xT[q * SQ:(q + 1) * SQ, :, :].rearrange("p a t -> p (a t)")
                                     .rearrange("p (n f) -> p n f", f=KC * RK)).then_inc(s_bst, 16)
                for c in range(NC):
                    if g - 2 < W_GROUPS:
                        sp.wait_ge(s_wt, KD * (g - 2) + KS * (c // 2 + 1))
                    else:
                        sp.wait_ge(s_bt, 4 * NC * (g - 2 - W_GROUPS) + 4 * (c + 1))
                    if g < W_GROUPS:
                        load_w(g, c)
                    elif g < X_GROUP0:
                        load_b(g, c)
                    else:
                        if g == X_GROUP0 + 1:
                            load_bsrc(1, c)
                        load_x(g - X_GROUP0, g % 2, c)
                if g in (3, 4):
                    sp.wait_ge(s_bst, 16 * NQ)
                    for c in range(2):
                        load_bsrc(0, 2 * (g - 3) + c)
                if g - 2 < W_GROUPS:
                    sp.wait_ge(s_glo, g - 2 + 1 + 2)
                    sp.dma_start(g_dram[:, :, (g - 2) * BANK:(g - 1) * BANK].rearrange("l p o -> p l o"),
                                 tmp[:, :, :]).then_inc(s_gst, 16)

            def step(b, f):
                if f is not None:
                    need(sp, s_acc, b.n * MT)
                    load_gm(f.n, f.q)
                for c in range(OC):
                    if f is None and c == OC - 1:
                        for t in range(NT):
                            sp.wait_ge(s_out, b.n * MT + NT * c + t + 1)
                            sp.dma_start(out_v[b.n, :, t, c * BANK:(c + 1) * BANK],
                                         xbuf[b.q][:, t, c * BANK:(c + 1) * BANK]).then_inc(s_store[c], 16)
                        continue
                    sp.wait_ge(s_out, b.n * MT + NT * (c + 1))
                    sp.dma_start(out_v[b.n, :, :, c * BANK:(c + 1) * BANK],
                                 xbuf[b.q][:, :, c * BANK:(c + 1) * BANK]).then_inc(s_store[c], 16)
                    if c > 0:
                        reload(b, c - 1)
                reload(b, OC - 1)

            def reload(b, c):
                if isinstance(b.n, int) and b.n + 2 >= NB:
                    return
                load_bsrc(b.n + 2, c)
                sp.wait_ge(s_store[c], b.n * 16 + 16)
                load_x(b.n + 2, b.q, c)

            step(Batch(0, 0), Batch(0, 1))
            with sp.Fori(0, NB // 2 - 2) as i:
                step(Batch(i, 1), Batch(i + 1, 0))
                step(Batch(i + 1, 0), Batch(i + 1, 1))
            h = NB // 2 - 2
            step(Batch(h, 1), Batch(h + 1, 0))
            step(Batch(h + 1, 0), Batch(h + 1, 1))
            step(Batch(h + 1, 1), None)
            for c in range(OC):
                sp.wait_ge(s_store[c], 16 * NB + (16 * (NT - 1) if c == OC - 1 else 0))

        @block.gpsimd
        def _(pool):
            pool.memset(ident[:, :], 0.0).then_inc(s_idn, 1)
            pool.wait_ge(s_idn, 1)
            pool.affine_select(out=ident[:, :], in_=ident[:, :], compare_op=ALU.not_equal, fill=1.0, base=0,
                               pattern=[[-1, P]], channel_multiplier=1).then_inc(s_idn, 1)
            pool.sem_inc(s_wlo, CREDIT)
            pool.sem_inc(s_wmm, CREDIT)
            pool.sem_inc(s_glo, 2)
            pool.sem_inc(s_gst, 16)
            fills = [(f32(gm_r[64:P, 0, :]), 0.0), (table[:, :, :], 0.0), (f32(sbx_r[64:P, :, :]), 1.0)]
            pool.wait_ge(s_idn, 2)
            for n, (where, value) in enumerate(fills):
                pool.memset(where, value).then_inc(s_const, 1)
                pool.wait_ge(s_const, n + 1)
            pool.iota(iota_e[:, :], [[1, E]], base=0, channel_multiplier=0,
                      allow_small_or_imprecise_dtypes=True).then_inc(s_iota, 1)
            pool.wait_ge(s_iota, 1)

            pool.wait_ge(s_bias, 32)
            for n, row in enumerate((64, 96)):
                pool.tensor_copy(gm_r[row:row + 1, 0, :], bias_n[row:row + 1, :]).then_inc(s_biashi, 1)
                pool.wait_ge(s_biashi, n + 1)
            pool.tensor_tensor(gm_r[96:97, 0, :], bias_n[96:97, :], f32(gm_r[96:97, 0, :]), ALU.subtract)\
                .then_inc(s_biaslo, 1)

            def take(f):
                pool.wait_ge(s_table, 3)
                need(pool, s_h, (f.n - 1) * 2 * OC)
                need(pool, s_lg, f.n - 1)
                pool.wait_ge(s_bd, f.n * NC + 2)
                pool.tensor_copy(cur[:, f.q, :], table[:, f.n, :]).then_inc(s_cur, 1)

            def diagonal(f, c):
                need(pool, s_bd, f.n * NC + c)
                if c == 2:
                    pool.wait_ge(s_cur, f.n + 1)
                pool.wait_ge(s_bsrc[c % 2], (f.n * 2 + c // 2) * 16 * NQ + 16 * NQ)
                need(pool, s_bxq, f.n * KD + KC * (c - 1))
                pool.tensor_tensor(bdiag[:, c % 2].rearrange("p j (q k) -> p j q k", q=NQ),
                                   bsrc[:, c % 2].rearrange("p (j k) -> p j k", k=RK).unsqueeze(2)
                                   .to_broadcast([P, NQ * KC, NQ, RK]),
                                   in_square[:, :].unsqueeze(1).unsqueeze(3).to_broadcast([P, NQ * KC, NQ, RK]),
                                   ALU.mult).then_inc(s_bd, 1)

            pool.wait_ge(s_biaslo, 1)
            pool.wait_ge(s_masks, 5)

            def prepare(f):
                for c in range(NC):
                    diagonal(f, c)
                    if c == 1:
                        take(f)

            prepare(Batch(0, 0))

            def step(b, f):
                if f is not None:
                    prepare(f)
            batches(pool, step)

        @block.scalar
        def _(act):
            def copy(dst, src):
                return act.activation(dst, src, ACT.Copy)

            def by_chunk(ap):
                return ap.rearrange("p b c s k -> p (c s) b k")

            act.dma_start(tok[:, :], itok.rearrange("(a b) -> a b", a=1)).then_inc(s_tok, 16)
            act.wait_ge(s_idn, 2)
            act.activation(mx[:, 0:1], ident[:, 0:1], ACT.Copy)
            act.wait_ge(s_tok, 16)
            load_adapters(act, 0)
            act.sem_inc(s_asked, 1)
            act.wait_ge(s_conda, 16 * NB)
            for c in range(NC):
                js = slice(c * KC, (c + 1) * KC)
                copy(a_r[:, 0, js, :].rearrange("p j (b k) -> p j b k", b=NB), by_chunk(conda_n)[:, js])\
                    .then_inc(s_ahi, 1)

            with act.Fori(0, W_GROUPS // 2) as i:
                for q in range(2):
                    g = i * 2 + q
                    for j in range(KD):
                        n = g * KD + j
                        act.wait_ge(s_wt, n + 1)
                        act.wait_ge(s_wmm, n - RING + 1 + CREDIT)
                        copy(wT_r[:, j % RING, 0, :], ps[:, j % RING, :]).then_inc(s_whi, 1)
                    act.wait_ge(s_wmm, (g + 1) * KD + CREDIT)
                    act.wait_ge(s_gst, g * 16 + 16)
                    copy(tmp[:, 0, :].bitcast(F32R), ps[:, ACC + q, :]).then_inc(s_ghi, 1)

            for n in range(B_RING):
                if B_BY[n] == "a":
                    copy_b(act, copy, n)

            def h_hi(b, c):
                for h in range(2):
                    act.wait_ge(s_h, (b.n * OC + c) * 2 + h + 1)
                    if h == 0:
                        need(act, s_acc, (b.n * OC + c - 1) * NT)
                    copy(h_r[:, c % 2, 0, h, :], ps[:, HB + h, :]).then_inc(s_hhi, 1)

            def slot(f, m):
                if m == EXP_AT:
                    act.wait_ge(s_lm, f.n + 1)
                    act.activation(ex[:, :, :], ex[:, :, :], ACT.Exp).then_inc(s_exp, 1)
                if m == SPREAD_AT:
                    act.wait_ge(s_rep, f.n + 1)
                    need(act, s_up, f.n * 2)
                    copy(bx[:, :], ps[:, BXB, :]).then_inc(s_bx, 1)
                    act.wait_ge(s_bx, f.n + 1)
                    need(act, s_acc, (f.n - 1) * MT)
                    copy(sbx_r[0:64, f.q, :], bx[0:64, :]).then_inc(s_sbhi, 1)
                if m == COMBK_AT:
                    act.wait_ge(s_comb, f.n + 1)
                    for a in range(2):
                        copy(combk[:, 2 * a:2 * a + 2].rearrange("p t e k -> p (t e) k"),
                             comb[:, 2 * a:2 * a + 2].rearrange("p t e -> p (t e)").unsqueeze(2)
                             .to_broadcast([P, 2 * E, RK])).then_inc(s_combk, 1)
                if m in UP_AT:
                    h = UP_AT[m]
                    act.wait_ge(s_up, f.n * 2 + h + 1)
                    copy(u_r[:, f.q, 0, h, :], tmp[:, h, :]).then_inc(s_uhi, 1)

            act.wait_ge(s_gst, 16 * (W_GROUPS + 1))
            first = Batch(0, 0)
            for m in range(MT):
                slot(first, m)
                for n in B_AT.get(m, ()):
                    if B_BY[n] == "a":
                        copy_b(act, copy, n)
                if m in H_AT:
                    h_hi(first, H_AT[m])

            def step(b, f):
                for c in range(OC):
                    if h_is_there(b, c + 1):
                        pass
                    elif c < OC - 1:
                        h_hi(b, c + 1)
                    elif f is not None:
                        h_hi(f, 0)
                    for t in range(NT):
                        if f is not None:
                            slot(f, c * NT + t)
            batches(act, step)

        @block.vector
        def _(dve):
            dve.wait_ge(s_idn, 2)
            dve.tensor_reduce(sum16, ident[:, :].rearrange("p (g k) -> p k g", k=RK), AX.X, ALU.add)\
               .then_inc(s_masks, 1)
            dve.tensor_reduce(sum8, ident[:, :].rearrange("p (g k) -> p g k", k=RK), AX.X, ALU.add).then_inc(s_masks, 1)
            dve.wait_ge(s_masks, 2)
            dve.tensor_copy(spread[:, :].rearrange("p (g k) -> p g k", k=RK),
                            sum16.unsqueeze(1).to_broadcast([P, P // RK, RK])).then_inc(s_masks, 1)
            dve.tensor_reduce(in_square[:, :], sum8.rearrange("p (q u) -> p q u", q=NQ), AX.X, ALU.add)\
               .then_inc(s_masks, 1)
            dve.tensor_tensor(in_block[:, :], sum8[:, 0:NQ], sum8[:, NQ:2 * NQ], ALU.add).then_inc(s_masks, 1)

            def small_copy(n):
                dve.wait_ge(s_st, n + 1)
                bank = ps[:, small_bank(n), :]
                if n < 4:
                    dst, src = ffnaT[:, 4 * n:4 * n + 4, :], bank.rearrange("p (j m) -> p j m", j=4)[:, :, 0:R + E]
                else:
                    dst, src = bT[:, 4 * (n - 4):4 * (n - 3)], bank.rearrange("p (j b k) -> p j b k", j=4, b=NB)
                dve.tensor_copy(dst, src).then_inc(s_se, 1)

            for n in range(4):
                small_copy(n)
            by_b = a_r[:, :, :, :].rearrange("p l j (b k) -> p l j b k", b=NB)
            for c in range(NC):
                js = slice(c * KC, (c + 1) * KC)
                dve.wait_ge(s_ahi, c + 1)
                dve.tensor_tensor(by_b[:, 1, js], conda_n.rearrange("p b c s k -> p (c s) b k")[:, js],
                                  f32(by_b[:, 0, js]), ALU.subtract).then_inc(s_alo, 1)

            for n in range(4, 8):
                small_copy(n)

            with dve.Fori(0, W_GROUPS // 2) as i:
                for q in range(2):
                    g = i * 2 + q
                    for j in range(KD):
                        n = g * KD + j
                        dve.wait_ge(s_whi, n + 1)
                        dve.tensor_tensor(wT_r[:, j % RING, 1, :], ps[:, j % RING, :],
                                          f32(wT_r[:, j % RING, 0, :]), ALU.subtract).then_inc(s_wlo, 1)
                    dve.wait_ge(s_ghi, g + 1)
                    dve.tensor_tensor(tmp[:, 1, :].bitcast(F32R), ps[:, ACC + q, :], tmp[:, 0, :], ALU.subtract)\
                       .then_inc(s_glo, 1)

            dve.wait_ge(s_const, 3)
            dve.wait_ge(s_bst, 16 * NQ)
            dve.wait_ge(s_sm, 1)
            ga = ps[:, MISC, 0:P].rearrange("p (b k) -> p b k", b=NB)
            for n in range(2):
                dve.tensor_scalar(table[n * R:(n + 1) * R, :, n * RK:(n + 1) * RK],
                                  ga[0:R], 0.5, None, ALU.mult).then_inc(s_table, 1)
            dve.tensor_copy(grT, ps[R:R + E, MISC, 0:P].rearrange("p (b k) -> p b k", b=NB).unsqueeze(2)
                            .to_broadcast([E, NB, P // RK, RK])).then_inc(s_grs, 1)

            for n in range(B_RING):
                if B_BY[n] == "d":
                    copy_b(dve, dve.tensor_copy, n)
                if n == GR_AFTER:
                    dve.wait_ge(s_sel, 1)
                    dve.tensor_copy(table[:, :, TB_R:TB_R + E],
                                    ps[:, BXB, 0:NB * E].rearrange("p (b e) -> p b e", b=NB))\
                       .then_inc(s_table, 1)

            def h_lo(b, c):
                for h in range(2):
                    dve.wait_ge(s_hhi, (b.n * OC + c) * 2 + h + 1)
                    dve.tensor_tensor(h_r[:, c % 2, 1, h, :], ps[:, HB + h, :], f32(h_r[:, c % 2, 0, h, :]),
                                      ALU.subtract).then_inc(s_hlo, 1)

            def slot(f, m):
                base = f.n * DVE_PER_FRONT
                at = {MAX_AT: 0, TOP_AT: 1, COMB_AT: 10}.get(m, 0)
                count = [at]

                def link(ins):
                    count[0] += 1
                    return ins.then_inc(s_dve, 1)

                def after(n=None):
                    dve.wait_ge(s_dve, base + (count[0] if n is None else n))

                def wide(ap):
                    return ap.unsqueeze(2).to_broadcast([P, NT, E])

                for j in T_AT.get(m, ()):
                    if j % 4 == 0:
                        dve.wait_ge(s_load[f.q][j // 4], load_count(f))
                    if j == 0:
                        need(dve, s_ct, f.n * 2)
                    need(dve, s_bxq, f.n * KD + j - RING + 1)
                    dve.transpose(xT[:, j % RING, :].rearrange("p (q t l) -> p t q l", q=NQ, t=NT),
                                  xbuf[f.q][:, :, j * P:(j + 1) * P]).then_inc(s_xe, 1)
                if m == BXP_AT:
                    dve.wait_ge(s_bxq, f.n * KD + KD)
                    need(dve, s_ulo, f.n * 2)
                    dve.tensor_tensor(bxp.rearrange("p (t q l) -> p t q l", t=NT, q=NQ),
                                      ps[:, BXB, 0:P].rearrange("p (t l) -> p t l", t=NT).unsqueeze(2)
                                      .to_broadcast([P, NT, NQ, SQ]),
                                      in_block[:, :].unsqueeze(1).unsqueeze(3).to_broadcast([P, NT, NQ, SQ]),
                                      ALU.mult).then_inc(s_bxp, 1)
                if m == MAX_AT:
                    dve.wait_ge(s_lg, f.n + 1)
                    lg = ps[:, MISC, 0:NT * E].rearrange("p (t e) -> p t e", t=NT)
                    link(dve.tensor_reduce(mx[:, :], lg, AX.X, ALU.max))
                    after()
                    dve.tensor_tensor(ex[:, :, :], lg, wide(mx[:, :]), ALU.subtract).then_inc(s_lm, 1)
                if m == TOP_AT:
                    dve.wait_ge(s_exp, f.n + 1)
                    link(dve.tensor_reduce(ssum[:, :], ex[:, :, :], AX.X, ALU.add))
                    after()
                    link(dve.reciprocal(rs[:, :], ssum[:, :]))
                    after()
                    link(dve.tensor_tensor(ex[:, :, :], ex[:, :, :], wide(rs[:, :]), ALU.mult))
                    after()
                    dve.sem_inc(s_gate, 1)
                    for t in range(NT):
                        link(dve.max(top[:, t, :], ex[:, t, :]))
                    after()
                    dve.sem_inc(s_gate, 1)
                    for t in range(NT):
                        ins = dve.max_index(topi[:, t, :], top[:, t, :], ex[:, t, :])
                        if t == NT - 1:
                            link(ins)
                    link(dve.scalar_tensor_tensor(out=rs[:, :], in0=top[:, :, 0], scalar=1e-6, in1=top[:, :, 1],
                                                  op0=ALU.add, op1=ALU.add))
                if m == COMB_AT:
                    after()
                    link(dve.reciprocal(ssum[:, :], rs[:, :]))
                    link(dve.tensor_copy(topf[:, :, :], topi[:, :, 0:2]))
                    after()
                    link(dve.tensor_tensor(wt2[:, :, :], top[:, :, 0:2],
                                           ssum[:, :].unsqueeze(2).to_broadcast([P, NT, 2]), ALU.mult))
                    iota_w = iota_e[:, :].unsqueeze(1).to_broadcast([P, NT, E])
                    for k in range(2):
                        link(dve.tensor_tensor(sel[:, :, k, :], iota_w, wide(topf[:, :, k]), ALU.is_equal))
                    after()
                    for k in range(2):
                        link(dve.tensor_tensor(sel[:, :, k, :], sel[:, :, k, :], wide(wt2[:, :, k]), ALU.mult))
                    after()
                    dve.tensor_tensor(comb[:, :, :], sel[:, :, 0, :], sel[:, :, 1, :], ALU.add).then_inc(s_comb, 1)
                if m == COMBK_AT:
                    dve.wait_ge(s_sbhi, f.n + 1)
                    dve.tensor_tensor(sbx_r[32:64, f.q, :], bx[32:64, :], f32(sbx_r[32:64, f.q, :]), ALU.subtract)\
                       .then_inc(s_sblo, 1)
                if m in UP_AT:
                    h = UP_AT[m]
                    dve.wait_ge(s_ct, f.n * 2 + h + 1)
                    need(dve, s_uhi, f.n * 2 - 2 + h + 1)
                    dve.tensor_tensor(tmp[:, h, :], ps[:, (MISC, BXB)[h], :], bx[:, :], ALU.mult).then_inc(s_up, 1)
                if m in LO_AT:
                    h = LO_AT[m]
                    dve.wait_ge(s_uhi, f.n * 2 + h + 1)
                    dve.tensor_tensor(u_r[:, f.q, 1, h, :], tmp[:, h, :], f32(u_r[:, f.q, 0, h, :]),
                                      ALU.subtract).then_inc(s_ulo, 1)

            first = Batch(0, 0)
            for m in range(MT):
                slot(first, m)
                for n in B_AT.get(m, ()):
                    if B_BY[n] == "d":
                        copy_b(dve, dve.tensor_copy, n)
                if m in H_AT:
                    h_lo(first, H_AT[m])

            def step(b, f):
                for c in range(OC):
                    if h_is_there(b, c + 1):
                        pass
                    elif c < OC - 1:
                        h_lo(b, c + 1)
                    elif f is not None:
                        h_lo(f, 0)
                    for t in range(NT):
                        m = c * NT + t
                        if f is not None and m == MT - 1:
                            slot(f, m)
                        dve.wait_ge(s_acc, b.n * MT + m + 1)
                        xs = xbuf[b.q][:, t, c * BANK:(c + 1) * BANK]
                        dve.tensor_tensor(xs, ps[:, ACC + t % 2, :], xs, ALU.add).then_inc(s_out, 1)
                        if f is not None and m < MT - 1:
                            slot(f, m)
            batches(dve, step)

        @block.tensor
        def _(pe):
            pe.wait_ge(s_idn, 2)

            def flip(bank, at, src, n=P):
                return pe.transpose(ps[:, bank, at:at + n], src, ident[0:n, 0:n])

            def w_transposes(q, j):
                c, s = j // KS, j % KS
                for t in range(NT):
                    src = xbuf[q][:, t, :].rearrange("p (c m s) -> p c s m", c=2, s=KS)[:, c, s, :]
                    ins = flip(j % RING, t * P, src)
                ins.then_inc(s_wt, 1)

            def w_products(q, g, j):
                n = g * KD + j
                pe.wait_ge(s_wlo, n + 1 + CREDIT)
                if j % KC == 0:
                    pe.wait_ge(s_alo, j // KC + 1)
                if j == 0:
                    pe.wait_ge(s_glo, g - 2 + 1 + 2)
                hi, lo = wT_r[:, j % RING, 0, :], wT_r[:, j % RING, 1, :]
                acc = ps[:, ACC + q, :]
                pe.matmul(acc, a_r[:, 0, j, :], hi, start=(j == 0), stop=False)
                pe.matmul(acc, a_r[:, 0, j, :], lo, start=False, stop=False)
                ins = pe.matmul(acc, a_r[:, 1, j, :], hi, start=False, stop=(j == KD - 1))
                ins.then_inc(s_wmm, 1)
                return ins

            pe.wait_ge(s_small, 32)
            by_s = ffna_n.rearrange("p (c m s) -> p c s m", c=2, s=KS)
            for n in range(4):
                for j in range(4):
                    jj = 4 * n + j
                    ins = flip(n, j * P, by_s[:, jj // KS, jj % KS, :], R + E)
                ins.then_inc(s_st, 1)
            pe.wait_ge(s_condb, 16 * NB)
            for n in range(4, 8):
                if n >= 6:
                    pe.wait_ge(s_se, n - 1)
                for j in range(4):
                    jj = 4 * (n - 4) + j
                    ins = flip(small_bank(n), j * P, condb_n[:, jj * P:(jj + 1) * P])
                ins.then_inc(s_st, 1)
            pe.wait_ge(s_se, 4)

            LEAD = 3
            with pe.Fori(0, W_GROUPS // 2) as i:
                for q in range(2):
                    g = i * 2 + q
                    for j in range(KD + LEAD):
                        if j < KD:
                            if j % KS == 0:
                                for c in range(2 * j // KS, 2 * j // KS + 2):
                                    pe.wait_ge(s_load[q][c], i * 16 + 16)
                            pe.wait_ge(s_wlo, g * KD + j - RING + 1 + CREDIT)
                            w_transposes(q, j)
                        if j >= LEAD:
                            w_products(q, g, j - LEAD)

            pe.wait_ge(s_conda, 16 * NB)
            for j in range(KD):
                a_j = conda_n[:, :, j // KS, j % KS, :]
                ins = pe.matmul(ps[0:R + E, MISC, 0:P], ffnaT[:, j, :], a_j, start=(j == 0), stop=(j == KD - 1))
            ins.then_inc(s_sm, 1)

            def b_transposes(n):
                g, c, s = n // (4 * NC), n // 4 % NC, n % 4
                if s == 0:
                    pe.wait_ge(s_load[g][c], 16 * (W_GROUPS // 2 + NT))
                before = [k for k in range(n) if b_bank(k) == b_bank(n)]
                if before:
                    b_copied(pe, before[-1])
                for u in range(4):
                    ins = flip(b_bank(n), u * P, xbuf[g][:, s, c * BANK + u * P:c * BANK + (u + 1) * P])
                ins.then_inc(s_bt, 1)

            def all_b_copied(n):
                for who in "ad":
                    b_copied(pe, B_BY[:n].rindex(who))

            for n in range(B_RING):
                b_transposes(n)
                if n == GR_AFTER:
                    pe.wait_ge(s_grs, 1)
                    for b in range(NB):
                        ins = pe.matmul(ps[:, BXB, b * E:(b + 1) * E], grT[:, b].rearrange("e g k -> e (g k)"),
                                        ident[0:E, 0:E], start=True, stop=True)
                    ins.then_inc(s_sel, 1)

            def h_products(b, c):
                pe.wait_ge(s_cur, b.n + 1)
                for h in range(2):
                    need(pe, s_hlo, (b.n * OC + c - 1) * 2 + h + 1)
                    for j in range(4):
                        ins = pe.matmul(ps[32 * j:32 * j + 32, HB + h, :], cur[:, b.q, 0:2 * RK],
                                        bexpT[:, 4 * h + j, c * BANK:(c + 1) * BANK], start=True, stop=True)
                    ins.then_inc(s_h, 1)

            def tile_products(b, c, t):
                m = c * NT + t
                acc = ps[:, ACC + t % 2, :]
                if m == 0:
                    pe.wait_ge(s_ulo, b.n * 2 + 2)
                    pe.wait_ge(s_sblo, b.n + 1)
                    pe.wait_ge(s_gm[b.q], b.half * 64 + 64)
                if t == 0:
                    pe.wait_ge(s_hlo, (b.n * OC + c) * 2 + 2)
                need(pe, s_out, b.n * MT + m - 1)
                tok_t = slice(t * P, (t + 1) * P)
                for h in range(2):
                    hi, lo = h_r[:, c % 2, 0, h, :], h_r[:, c % 2, 1, h, :]
                    pe.matmul(acc, u_r[:, b.q, 0, h, tok_t], hi, start=(h == 0), stop=False)
                    pe.matmul(acc, u_r[:, b.q, 0, h, tok_t], lo, start=False, stop=False)
                    pe.matmul(acc, u_r[:, b.q, 1, h, tok_t], hi, start=False, stop=False)
                pe.matmul(acc, sbx_r[:, b.q, tok_t], gm_r[:, b.q, c * BANK:(c + 1) * BANK], start=False, stop=True)\
                  .then_inc(s_acc, 1)

            def slot(f, m):
                for j in Q_AT.get(m, ()):
                    if j % KC == 0:
                        pe.wait_ge(s_bd, f.n * NC + j // KC + 1)
                    if j == 0:
                        need(pe, s_up, f.n * 2)
                    pe.wait_ge(s_xe, f.n * KD + j + 1)
                    for q in range(NQ):
                        half = (q % 2) * NQ * RK
                        ins = pe.matmul(ps[half:half + NQ * RK, BXB, 0:P], bdiag[:, j // KC % 2, q * KC + j % KC, :],
                                        xT[:, j % RING, q * P:(q + 1) * P],
                                        start=(j == 0 and q < 2), stop=(j == KD - 1 and q >= 2))
                    ins.then_inc(s_bxq, 1)
                if m == SPREAD_AT:
                    pe.wait_ge(s_bxp, f.n + 1)
                    pe.wait_ge(s_cur, f.n + 1)
                    for t in range(NT):
                        ins = pe.matmul(ps[:, MISC, t * E:(t + 1) * E], bxp[:, t * P:(t + 1) * P],
                                        cur[:, f.q, TB_R:TB_R + E], start=True, stop=True)
                    ins.then_inc(s_lg, 1)
                    pe.matmul(ps[:, BXB, :], spread[:, :], bxp,
                              start=True, stop=True).then_inc(s_rep, 1)
                if m in CT_AT:
                    h = CT_AT[m]
                    pe.wait_ge(s_combk, f.n * 2 + 2)
                    if h == 1:
                        pe.wait_ge(s_bx, f.n + 1)
                    for t in range(NT):
                        w = combk[:, t, h * EH:(h + 1) * EH, :].rearrange("p e k -> p (e k)")
                        ins = flip((MISC, BXB)[h], t * P, w)
                    ins.then_inc(s_ct, 1)

            pe.wait_ge(s_glo, W_GROUPS + 2)
            pe.wait_ge(s_masks, 5)
            pe.wait_ge(s_bias, 48)
            first = Batch(0, 0)
            for m in range(MT):
                slot(first, m)
                for n in B_AT.get(m, ()):
                    b_transposes(n)
                if m in H_AT:
                    all_b_copied(B_RING)
                    h_products(first, H_AT[m])

            def step(b, f):
                for c in range(OC):
                    if h_is_there(b, c + 1):
                        pass
                    elif c < OC - 1:
                        h_products(b, c + 1)
                    elif f is not None:
                        h_products(f, 0)
                    for t in range(NT):
                        tile_products(b, c, t)
                        if f is not None:
                            slot(f, c * NT + t)
            all_b_copied(2 * B_RING)
            batches(pe, step)


_INS = ["x", "itok_B_3_7", "L0_cond_A", "L0_cond_B", "L0_ffn_base_w", "L0_ffn_base_b", "L0_ffn_A", "L0_ffn_B",
        "L0_ffn_router_w"]


def kernel(**inputs):
    import numpy as np
    import concourse.bacc as bacc
    from concourse.bass_utils import run_bass_kernel_spmd

    nc = bacc.Bacc("TRN2", target_bir_lowering=False, num_devices=1)
    arrays, args = {}, []
    for name in _INS:
        a = np.ascontiguousarray(inputs[name])
        arrays[f"in_{name}"] = a
        args.append(nc.dram_tensor(f"in_{name}", a.shape, mybir.dt.from_np(a.dtype), kind="ExternalInput").ap())
    shape = inputs["x"].shape
    args.append(nc.dram_tensor("out_0", shape, F32, kind="ExternalOutput").ap())
    adaln_ffn(nc, *args)
    r = run_bass_kernel_spmd(nc, [arrays], core_ids=[0])
    return r.results[0]["out_0"]
```
